# Optimizing a Trainium2 kernel written in Bass

```python
import numpy as np
import jax
import jax.numpy as jnp

def _softmax(x, axis=-1):
    return jax.nn.softmax(x, axis=axis)
def _gelu(x):
    return jax.nn.gelu(x, approximate=True)
def _silu(x):
    return jax.nn.silu(x)
def _sigmoid(x):
    return jax.nn.sigmoid(x)
def _layernorm(x, axis=-1, eps=1e-5):
    m = jnp.mean(x, axis=axis, keepdims=True)
    v = jnp.var(x, axis=axis, keepdims=True)
    return (x - m) / jnp.sqrt(v + eps)
def _scatter_add(tgt, idx, src, axis=0):
    return tgt.at[idx].add(src)
def _segment_sum(src, seg, n):
    return jax.ops.segment_sum(src, seg, n)

kernel_name = 'mk_conv_preact_d4_conv_nhwc256_4b056c'

def setup_inputs(seed: int = 0):
    np.random.seed(seed)
    _w = jnp.asarray
    def _rec_inputs():
        import jax
        import jax.numpy as jnp
        _gk = jax.random.key(seed)
        x = -0.0003929 + 0.9999 * jax.random.normal(jax.random.fold_in(_gk, 1), (16, 64, 64, 256), jnp.float32)
        return x
    x = _rec_inputs()
    def _L0_conv_setup():
        import jax, jax.numpy as jnp
        import numpy as np

        def encode(x, embeddings):
            xf = x.reshape(-1, x.shape[-1])
            dis = jnp.sum(xf * xf, axis=-1, keepdims=True) + jnp.sum(embeddings * embeddings, axis=0, keepdims=True) - 2.0 * jnp.matmul(xf, embeddings)
            indices = jnp.argmin(dis, axis=-1)
            return indices.reshape(x.shape[:-1])

        def decode(indices, embeddings):
            return jnp.take(embeddings.T, indices, axis=0)
        key = jax.random.key(seed)
        k1, k2 = jax.random.split(key)
        B, H, W, D, K = (16, 64, 64, 256, 1024)
        x = jax.random.normal(k1, (B, H, W, D), dtype=jnp.float32)
        limit = np.sqrt(3.0 / D).astype(np.float32)
        embeddings = jax.random.uniform(k2, (D, K), dtype=jnp.float32, minval=-limit, maxval=limit)
        return {'x': x, 'embeddings': embeddings}
    _L0_conv_all = _L0_conv_setup()
    _L0_conv_in = {k: v for k, v in _L0_conv_all.items() if k in ('embeddings', )}
    del _L0_conv_all

    def _L1_conv_setup():
        import jax, jax.numpy as jnp
        import numpy as np
        key = jax.random.key(seed)
        ks = jax.random.split(key, 4)
        B, H, W, C = (4, 256, 256, 256)
        Ck = C // 8
        x = jax.random.normal(ks[0], (B, H, W, C), dtype=jnp.float32)
        Wf = jax.random.normal(ks[1], (C, Ck), dtype=jnp.float32) / np.sqrt(C)
        Wg = jax.random.normal(ks[2], (C, Ck), dtype=jnp.float32) / np.sqrt(C)
        Wh = jax.random.normal(ks[3], (C, C), dtype=jnp.float32) / np.sqrt(C)
        bf = jnp.zeros((Ck,), jnp.float32)
        bg = jnp.zeros((Ck,), jnp.float32)
        bh = jnp.zeros((C,), jnp.float32)
        return {'x': x, 'Wf': Wf, 'bf': bf, 'Wg': Wg, 'bg': bg, 'Wh': Wh, 'bh': bh}
    _L1_conv_all = _L1_conv_setup()
    _L1_conv_in = {k: v for k, v in _L1_conv_all.items() if k in ('Wf', 'bf', 'Wg', 'bg', 'Wh', 'bh', )}
    del _L1_conv_all

    def _L2_conv_setup():
        import jax, jax.numpy as jnp
        import numpy as np
        B, H, W, C = (16, 64, 64, 256)
        key = jax.random.key(seed)
        ks = jax.random.split(key, 4)
        x = jax.random.normal(ks[0], (B, H, W, C), dtype=jnp.float32)
        w1 = jax.random.normal(ks[1], (C,), dtype=jnp.float32) * C ** (-0.5)
        w2 = jax.random.normal(ks[2], (C,), dtype=jnp.float32) * C ** (-0.5)
        w3 = jax.random.normal(ks[3], (C,), dtype=jnp.float32) * C ** (-0.5)
        b1 = jnp.zeros((1,), jnp.float32)
        b2 = jnp.zeros((1,), jnp.float32)
        b3 = jnp.zeros((1,), jnp.float32)
        return {'x': x, 'w1': w1, 'b1': b1, 'w2': w2, 'b2': b2, 'w3': w3, 'b3': b3}
    _L2_conv_all = _L2_conv_setup()
    _L2_conv_in = {k: v for k, v in _L2_conv_all.items() if k in ('w1', 'b1', 'w2', 'b2', 'w3', 'b3', )}
    del _L2_conv_all

    def _L3_conv_setup():
        import jax, jax.numpy as jnp
        import numpy as np
        HEADS = 4
        DIM_HEAD = 32
        SCALE = DIM_HEAD ** (-0.5)
        LN_EPS = 0.001
        key = jax.random.key(seed)
        ks = jax.random.split(key, 3)
        B, H, W, C = (16, 64, 64, 256)
        hidden = HEADS * DIM_HEAD
        x = jax.random.normal(ks[0], (B, H, W, C), dtype=jnp.float32)
        w_qkv = jax.random.normal(ks[1], (C, 3 * hidden), dtype=jnp.float32) * C ** (-0.5)
        w_out = jax.random.normal(ks[2], (hidden, C), dtype=jnp.float32) * hidden ** (-0.5)
        b_out = jnp.zeros((C,), dtype=jnp.float32)
        gamma = jnp.ones((C,), dtype=jnp.float32)
        beta = jnp.zeros((C,), dtype=jnp.float32)
        return {'x': x, 'w_qkv': w_qkv, 'w_out': w_out, 'b_out': b_out, 'gamma': gamma, 'beta': beta}
    _L3_conv_all = _L3_conv_setup()
    _L3_conv_in = {k: v for k, v in _L3_conv_all.items() if k in ('w_qkv', 'w_out', 'b_out', 'gamma', 'beta', )}
    del _L3_conv_all

    return {
        "x": x,
        "L0_conv_embeddings": _L0_conv_in["embeddings"],
        "L1_conv_Wf": _L1_conv_in["Wf"],
        "L1_conv_bf": _L1_conv_in["bf"],
        "L1_conv_Wg": _L1_conv_in["Wg"],
        "L1_conv_bg": _L1_conv_in["bg"],
        "L1_conv_Wh": _L1_conv_in["Wh"],
        "L1_conv_bh": _L1_conv_in["bh"],
        "L2_conv_w1": _L2_conv_in["w1"],
        "L2_conv_b1": _L2_conv_in["b1"],
        "L2_conv_w2": _L2_conv_in["w2"],
        "L2_conv_b2": _L2_conv_in["b2"],
        "L2_conv_w3": _L2_conv_in["w3"],
        "L2_conv_b3": _L2_conv_in["b3"],
        "L3_conv_w_qkv": _L3_conv_in["w_qkv"],
        "L3_conv_w_out": _L3_conv_in["w_out"],
        "L3_conv_b_out": _L3_conv_in["b_out"],
        "L3_conv_gamma": _L3_conv_in["gamma"],
        "L3_conv_beta": _L3_conv_in["beta"],
    }

def reference(x, L0_conv_embeddings, L1_conv_Wf, L1_conv_bf, L1_conv_Wg, L1_conv_bg, L1_conv_Wh, L1_conv_bh, L2_conv_w1, L2_conv_b1, L2_conv_w2, L2_conv_b2, L2_conv_w3, L2_conv_b3, L3_conv_w_qkv, L3_conv_w_out, L3_conv_b_out, L3_conv_gamma, L3_conv_beta):
    import jax
    import jax.numpy as jnp
    def _L0_conv_ref(x, embeddings):
        import jax, jax.numpy as jnp
        import numpy as np

        def encode(x, embeddings):
            xf = x.reshape(-1, x.shape[-1])
            dis = jnp.sum(xf * xf, axis=-1, keepdims=True) + jnp.sum(embeddings * embeddings, axis=0, keepdims=True) - 2.0 * jnp.matmul(xf, embeddings)
            indices = jnp.argmin(dis, axis=-1)
            return indices.reshape(x.shape[:-1])

        def decode(indices, embeddings):
            return jnp.take(embeddings.T, indices, axis=0)
        indices = encode(x, embeddings)
        quantized = decode(indices, embeddings)
        return quantized

    def _L1_conv_ref(x, Wf, bf, Wg, bg, Wh, bh):
        import jax, jax.numpy as jnp
        import numpy as np
        f = jnp.einsum('bhwc,ck->bhwk', x, Wf) + bf
        g = jnp.einsum('bhwc,ck->bhwk', x, Wg) + bg
        h = jnp.einsum('bhwc,co->bhwo', x, Wh) + bh
        scores = jnp.einsum('bhik,bhjk->bhij', f, g)
        attn = jax.nn.sigmoid(scores)
        out = jnp.einsum('bhij,bhjo->bhio', attn, h)
        return out

    def _L2_conv_ref(x, w1, b1, w2, b2, w3, b3):
        import jax, jax.numpy as jnp
        import numpy as np
        B, H, W, C = (16, 64, 64, 256)
        b, h, w, c = x.shape
        n = h * w
        xf = x.reshape(b, n, c)
        x0 = jnp.einsum('bnc,c->bn', xf, w1) + b1[0]
        x1 = jnp.einsum('bnc,c->bn', xf, w2) + b2[0]
        x2 = jnp.einsum('bnc,c->bn', xf, w3) + b3[0]
        sim = x0[:, :, None] * x1[:, None, :]
        sm = jax.nn.softmax(sim, axis=1)
        feats = jnp.einsum('bn,bnm->bm', x2, sm)
        gate = jax.nn.sigmoid(feats).reshape(b, h, w, 1)
        return gate * x

    def _L3_conv_ref(x, w_qkv, w_out, b_out, gamma, beta):
        import jax, jax.numpy as jnp
        import numpy as np
        HEADS = 4
        DIM_HEAD = 32
        SCALE = DIM_HEAD ** (-0.5)
        LN_EPS = 0.001
        B, H, W, C = x.shape
        n = H * W
        qkv = jnp.einsum('bxyc,cf->bxyf', x, w_qkv)
        q, k, v = jnp.split(qkv, 3, axis=-1)

        def to_bhcn(t):
            t = t.reshape(B, H, W, HEADS, DIM_HEAD)
            return t.transpose(0, 3, 4, 1, 2).reshape(B, HEADS, DIM_HEAD, n)
        q, k, v = (to_bhcn(q), to_bhcn(k), to_bhcn(v))
        q = jax.nn.softmax(q, axis=-2) * SCALE
        k = jax.nn.softmax(k, axis=-1)
        context = jnp.einsum('bhdn,bhen->bhde', k, v)
        out = jnp.einsum('bhde,bhdn->bhen', context, q)
        out = out.reshape(B, HEADS, DIM_HEAD, H, W).transpose(0, 3, 4, 1, 2)
        out = out.reshape(B, H, W, HEADS * DIM_HEAD)
        out = jnp.einsum('bxyh,hc->bxyc', out, w_out) + b_out
        mu = jnp.mean(out, axis=-1, keepdims=True)
        var = jnp.mean(jnp.square(out - mu), axis=-1, keepdims=True)
        out = (out - mu) * jax.lax.rsqrt(var + LN_EPS) * gamma + beta
        return out

    def _gn(v, G=32, eps=1e-5):
        B_, H_, W_, C_ = v.shape
        g = v.reshape(B_, H_, W_, G, C_ // G)
        m = jnp.mean(g, axis=(1, 2, 4), keepdims=True)
        s = jnp.var(g, axis=(1, 2, 4), keepdims=True)
        return ((g - m) / jnp.sqrt(s + eps)).reshape(v.shape)

    def _ln_c(v, eps=1e-6):
        m = jnp.mean(v, axis=-1, keepdims=True)
        s = jnp.var(v, axis=-1, keepdims=True)
        return (v - m) / jnp.sqrt(s + eps)

    def _ln_t(v, eps=1e-5):
        m = jnp.mean(v, axis=-1, keepdims=True)
        s = jnp.var(v, axis=-1, keepdims=True)
        return (v - m) / jnp.sqrt(s + eps)

    def _to_tokens(v):
        B_, H_, W_, C_ = v.shape
        return v.reshape(B_, H_ * W_, C_)
    def _from_tokens(t, like):
        return t.reshape(like.shape)

    x = x + _L0_conv_ref(_gn(x), L0_conv_embeddings)
    x = x + _L1_conv_ref(_gn(x), L1_conv_Wf, L1_conv_bf, L1_conv_Wg, L1_conv_bg, L1_conv_Wh, L1_conv_bh)
    x = x + _L2_conv_ref(_gn(x), L2_conv_w1, L2_conv_b1, L2_conv_w2, L2_conv_b2, L2_conv_w3, L2_conv_b3)
    x = x + _L3_conv_ref(_gn(x), L3_conv_w_qkv, L3_conv_w_out, L3_conv_b_out, L3_conv_gamma, L3_conv_beta)
    return x


_drawn_inputs = setup_inputs


def setup_inputs(seed=0):
    import zlib

    import numpy as np

    out = dict(_drawn_inputs(seed))
    spreads = {'L1_conv_bf': (0.0, 0.1),
     'L1_conv_bg': (0.0, 0.1),
     'L1_conv_bh': (0.0, 0.1),
     'L3_conv_b_out': (0.0, 0.1),
     'L3_conv_gamma': (1.0, 0.2),
     'L3_conv_beta': (0.0, 0.515)}
    factors = {'L2_conv_w1': 8.0, 'L2_conv_w2': 8.0, 'L2_conv_w3': 8.0}
    for name, (base, spread) in spreads.items():
        noise = np.random.default_rng([zlib.crc32(name.encode()), seed]).standard_normal(out[name].shape)
        drawn = base * np.exp(spread * noise) if base else spread * noise
        out[name] = jnp.asarray(drawn.astype(out[name].dtype))
    for name, factor in factors.items():
        out[name] = (out[name] * factor).astype(out[name].dtype)
    return out
```

```python
from contextlib import ExitStack

import concourse.bass as bass
from concourse import mybir

F32 = mybir.dt.float32
F16 = mybir.dt.float16
BF16 = mybir.dt.bfloat16
U32 = mybir.dt.uint32
ALU = mybir.AluOpType
ACT = mybir.ActivationFunctionType
AX = mybir.AxisListType.X

P = 128
KC = 2
C = KC * P
GT = 4
GW = GT * P
NG = 8
NT = NG * GT
N = NG * GW
CODES = 1024
CK = 32
ROW = 64
HEADS = 4
DH = 32
HID = HEADS * DH
GN_GROUP = C // 32
GN_EPS = 1e-5
LN_EPS = 1e-3
PIECES = 12
BROW = 32
NHALF = 2
UNIT = N // NHALF
ZW = 1024
ZONES = 3
QUADS = 4
TRIO = 3
KAPPA = 256.0


class Step:

    def __init__(self, nc, ctx, name, depth=0):
        self.sem = ctx.enter_context(nc.semaphore(name))
        self.depth = depth

    def after(self, n):
        return n + (self.depth + 1)

    def room(self, n, depth=None):
        return n + 1 + (0 if depth is None else self.depth - depth)


class Group:

    def __init__(self, im, i, c):
        self.slot = c % 2
        self.pair = i + c // 2
        self.n = im * NG + i * 2 + c
        self.occ = im * (NG // 2) + i + c // 2


def pipeline(eng, im, stages, step):

    def static(k):
        return lambda s: Group(im, 0, k - s) if 0 <= k - s < NG else None

    for k in range(2):
        step(static(k))
    with eng.Fori(0, (NG - 2) // 2) as i:
        for u in range(2):
            step(lambda s, u=u: Group(im, i, 2 + u - s))
    for k in range(NG, NG + stages - 1):
        step(static(k))


class Chain:

    def __init__(self, sem, per):
        self.sem, self.per, self.k = sem, per, 0

    def start(self, rnd):
        self.rnd, self.k = rnd, 0

    def link(self, eng, ins):
        self.k += 1
        ins.then_inc(self.sem, 1)
        eng.wait_ge(self.sem, self.rnd * self.per + self.k)

    def end(self):
        assert self.k == self.per, (self.k, self.per)


def build(nc, x, emb, emb_t, wfg, bfg, wh, bh, w3, b3, wqv, wk, w_out, b_out, gamma, beta, ident_in, gmat_in, out):
    B = x.shape[0]
    xv = x.rearrange("b (g u r) w c -> b g (r w) u c", g=NG, u=GT)
    ov = out.rearrange("b (q s u r) w c -> b (r w) q s u c", q=NG // 2, s=2, u=GT)

    with ExitStack() as ctx:
        def sb(name, shape, dt=F32):
            return ctx.enter_context(nc.sbuf_tensor(name, shape, dt))

        def sem(name):
            return ctx.enter_context(nc.semaphore(name))

        def step(name, depth=0):
            s = Step(nc, ctx, name, depth)
            if depth:
                credited.append(s)
            return s

        credited = []
        PS = ctx.enter_context(nc.psum_tensor("PS", [P, 8, 512], F32))

        ident = sb("ident", [P, P])
        gmat = sb("gmat", [P, P])
        ones = sb("ones", [P, P])
        minus_half = sb("minus_half", [P, 96])
        onesel = sb("onesel", [96, 512], BF16)
        mhalf2 = sb("mhalf2", [P, GT])
        e_hi = sb("e_hi", [P, KC, CODES], F16)
        e_lo = sb("e_lo", [P, KC, CODES], F16)
        e_bias = sb("e_bias", [96, CODES], BF16)
        fg_hi = sb("fg_hi", [P, KC, 2 * CK], F16)
        fg_lo = sb("fg_lo", [P, KC, 2 * CK], F16)
        fg_bias = sb("fg_bias", [96, 2 * CK], BF16)
        h_hi = sb("h_hi", [P, KC, C], F16)
        h_lo = sb("h_lo", [P, KC, C], F16)
        h_bias = sb("h_bias", [P, C])
        w3_sb = sb("w3_sb", [P, KC, 3])
        b3_sb = sb("b3_sb", [P, 3])
        qv_hi = sb("qv_hi", [P, KC, 2 * HID], F16)
        qv_lo = sb("qv_lo", [P, KC, 2 * HID], F16)
        k_hi = sb("k_hi", [P, KC, HID], F16)
        k_lo = sb("k_lo", [P, KC, HID], F16)
        wo_c = sb("wo_c", [P, C])
        z_bias = sb("z_bias", [96, C], BF16)
        gamma_b = sb("gamma_b", [P, C])
        beta_c = sb("beta_c", [P, KC])

        xin = sb("xin", [P, NG, GT, C])
        XT = sb("XT", [P, KC, NG // 2, 2, GW])
        xn = sb("xn", [P, 2, KC, GW])
        xhi = sb("xhi", [P, 2, KC, GW], F16)
        xlo = sb("xlo", [P, 2, KC, GW], F16)

        stats = sb("stats", [P, KC, NG // 2, 2, 6])
        mv = sb("mv", [P, KC, 2])
        gm = sb("gm", [P, KC])
        dm = sb("dm", [P, KC])
        vv = sb("vv", [P, KC])
        ve = sb("ve", [P, KC])
        gs = sb("gs", [P, KC])
        gt = sb("gt", [P, KC])
        m8 = sb("m8", [P, 2, 8])
        idx = sb("idx", [P, 2 * GT, 8], U32)

        work = sb("work", [P, 6144])
        quant = work[:, 0:2048].rearrange("p (s u c) -> p s u c", s=2, u=GT)
        H = work[:, 0:2048].rearrange("p (s u c) -> p s u c", s=2, u=GT)
        FT = work[0:CK, 2048:3072].rearrange("p (s n) -> p s n", s=2)
        GTm = work[0:CK, 3072:4096].rearrange("p (s n) -> p s n", s=2)
        diag = work[:, 0:1024].rearrange("p (s u n) -> p s u n", s=2, u=GT)
        gated = work[:, 1024:3072].rearrange("p (s k n) -> p s k n", s=2, k=KC)
        qe = work[:, 0:1024].rearrange("p (s u n) -> p s u n", s=2, u=GT)
        qs = work[:, 1024:2048].rearrange("p (s u n) -> p s u n", s=2, u=GT)
        ke = work[:, 2048:3072].rearrange("p (s u n) -> p s u n", s=2, u=GT)
        kt = work[:, 3072:4096].rearrange("p (s u n) -> p s u n", s=2, u=GT)
        xb = work[:, 0:2048].rearrange("p (s k n) -> p s k n", s=2, k=KC)
        Y = work[:, 2048:4096].rearrange("p (s u c) -> p s u c", s=2, u=GT)
        squares = work[:, 4096:6144].rearrange("p (s u c) -> p s u c", s=2, u=GT)
        attn = sb("attn", [P, 2, GT, P])
        yout = sb("yout", [P, 2, GT, C])

        big = sb("big", [P, 12288])
        E = big[:, 0:TRIO * 2048].rearrange("p (s n) -> p s n", s=TRIO)
        lhs_p = big[0:PIECES, 6144:8192].bitcast(BF16)
        rhs_p = big[0:PIECES, 8192:10240].bitcast(BF16)
        pc = big[:, 10240:10240 + NT * 44].rearrange("p (t k) -> p t k", k=44)
        accs = big[:, 0:1024]
        KTs = big[:, 0:4096].rearrange("p (g s n) -> p g s n", g=NG // 2, s=2)
        V = big[:, 4096:8192].rearrange("p (g s u n) -> p g s u n", g=NG // 2, s=2, u=GT)
        q_hi = big[:, 8192:10240].bitcast(F16).rearrange("p (g s u n) -> p g s u n", g=NG // 2, s=2, u=GT)
        q_lo = big[:, 10240:12288].bitcast(F16).rearrange("p (g s u n) -> p g s u n", g=NG // 2, s=2, u=GT)

        s3 = sb("s3", [P, 3, NT])
        x2c = sb("x2c", [P, NT])
        pk = sb("pk", [P, 3, 3, NT], BF16)
        r3 = sb("r3", [P, 2, 3, NT])
        mm2 = sb("mm2", [P, 2])
        mt2 = sb("mt2", [2, 1])
        dg2 = sb("dg2", [2, 2])
        mx2 = sb("mx2", [P, 2])
        ma = sb("ma", [P, 2, NT])
        lhs_s = sb("lhs_s", [PIECES, TRIO, P], BF16)
        w2 = sb("w2", [P, TRIO, 32])
        zero_w = sb("zero_w", [P, P])
        gate = sb("gate", [P, 3, NT])
        nums = sb("nums", [P, NHALF, QUADS, GT])
        qmx = sb("qmx", [P, 2, GT * HEADS])
        qsum = sb("qsum", [P, 2, 2, GT * HEADS])
        kmx = sb("kmx", [P, NG // 2, 2])
        kneg = sb("kneg", [P, 1])
        ksum = sb("ksum", [P, NG // 2, 2])
        kden = sb("kden", [P, 2])
        ctxd = sb("ctxd", [P, P])
        ctxt = sb("ctxt", [P, P])
        m_hi = sb("m_hi", [P, C], F16)
        m_lo = sb("m_lo", [P, C], F16)
        sq = sb("sq", [P, 2, GT])
        rstd = sb("rstd", [P, 2, 2, GT])

        weights_in = sem("weights_in")
        setup_dve = sem("setup_dve")
        emb_squared = sem("emb_squared")
        setup_pe = sem("setup_pe")
        start = sem("start")
        phase_end = sem("phase_end")
        waits_apart = sem("waits_apart")
        loaded = [sem(f"loaded{g}") for g in range(NG)]
        gathered = [[sem(f"gathered{s}{u}") for u in range(GT)] for s in range(2)]
        stored = [sem(f"stored{s}") for s in range(2)]
        a_turned = step("a_turned", 8)
        a_kept = step("a_kept", 2)
        stats_done = [step(f"stats_done{l}") for l in range(4)]
        mean_ready, mean_ps, var_ready, var_ps, ve_ready, pow_done, gn_ready = (
            step(n) for n in ("mean_ready", "mean_ps", "var_ready", "var_ps", "ve_ready", "pow_done", "gn_ready"))
        l0_xn, l0_hi, l0_lo = step("l0_xn"), step("l0_hi"), step("l0_lo", 2)
        l0_scored, l0_maxed, l0_indexed = step("l0_scored", 8), step("l0_maxed"), step("l0_indexed", 2)
        l0_turned, l0_added = step("l0_turned", 2), step("l0_added", 2)
        l1_xn, l1_hi, l1_lo = step("l1_xn"), step("l1_hi"), step("l1_lo", 2)
        l1_fg, l1_fgkept, l1_h, l1_hkept = step("l1_fg"), step("l1_fgkept", 2), step("l1_h", 4), step("l1_hkept", 2)
        l1_scores, l1_attn = step("l1_scores", 2), step("l1_attn", 2)
        l1_out, l1_added = step("l1_out", 2), step("l1_added", 1)
        l2_xn, l2_proj = step("l2_xn"), step("l2_proj", 2)
        x0max_in, x0max_t, x0max_d, x0max_b = (step(n) for n in ("x0max_in", "x0max_t", "x0max_d", "x0max_b"))
        pieces_made, pieces_turned, pieces_kept = step("pieces_made"), step("pieces_turned"), step("pieces_kept", 2)
        exps_in, exps_done, sums_done = step("exps_in"), step("exps_done", ZONES), step("sums_done", 6)
        tile_staged = step("tile_staged")
        acc_kept, acc_turned = step("acc_kept"), step("acc_turned")
        gate_exp, gate_made = step("gate_exp"), step("gate_made")
        g_xn, g_diag, g_spread = step("g_xn"), step("g_diag"), step("g_spread", 2)
        g_gated, g_added = step("g_gated", 2), step("g_added", 2)
        l3_xn, l3_hi, l3_lo = step("l3_xn"), step("l3_hi"), step("l3_lo", 2)
        l3_k, l3_kkept, l3_kmax = step("l3_k"), step("l3_kkept", 2), step("l3_kmax", 2)
        l3_qv, l3_vkept = step("l3_qv", 2), step("l3_vkept", 2)
        l3_qsub, l3_qexp, l3_qsoft = step("l3_qsub", 2), step("l3_qexp", 2), step("l3_qsoft")
        l3_qt, l3_qhi, l3_qlo = step("l3_qt", 2), step("l3_qhi", 2), step("l3_qlo", 2)
        kneg_ready, l3_kexp, l3_kturned, l3_kback = step("kneg_ready"), step("l3_kexp"), step("l3_kturned", 2), step("l3_kback", 2)
        l3_ctx, ctx_done, ctxd_ready, ctxt_ps, ctxt_ready, m_ps, mhi_ready, mlo_ready = (
            step("l3_ctx", 2), *(step(n) for n in ("ctx_done", "ctxd_ready", "ctxt_ps", "ctxt_ready", "m_ps", "mhi_ready", "mlo_ready")))
        f_xb, f_turned, f_z, f_sq = step("f_xb"), step("f_turned", 2), step("f_z"), step("f_sq", 2)
        f_ve, f_rstd, f_y, f_out = step("f_ve"), step("f_rstd"), step("f_y", 2), step("f_out", 2)
        gn_chain = Chain(sem("gn_chain"), 4)
        small_chain = Chain(sem("small_chain"), 10)
        gate_chain = Chain(sem("gate_chain"), 4)
        q_chain = Chain(sem("q_chain"), 3)
        k_chain = Chain(sem("k_chain"), 3)

        PHASES = 9
        block = ctx.enter_context(nc.Block())

        def qv_ps(g):
            return PS[:, 2 + 2 * g.slot:4 + 2 * g.slot, :].rearrange("p a (u n) -> p (a u) n", u=2)

        def z_ps(g):
            return PS[:, 2 * g.slot:2 * g.slot + 2, :].rearrange("p a (u n) -> p (a u) n", u=2)

        def xt_ps(g):
            return PS[:, 4 + 2 * g.slot:6 + 2 * g.slot, :].rearrange("p a (u n) -> p (a u) n", u=2)

        def apart(eng):
            eng.sem_inc(waits_apart, 1)

        def barrier(eng, im, phase):
            apart(eng)
            eng.drain().then_inc(phase_end, 1)
            eng.wait_ge(phase_end, im * (4 * PHASES) + 4 * (phase + 1))
            apart(eng)

        wst = xin[:, :, :, :].rearrange("p g u c -> p (g u c)")
        emb_f = wst[:, 0:2048].rearrange("p (k n) -> p k n", k=KC)
        emb_q = wst[:, 2048:4096].rearrange("p (k n) -> p k n", k=KC)
        wfg_f = XT[:, 0, 0, 0, 0:128].rearrange("p (k n) -> p k n", k=KC)
        xt_w = XT[:, :, :, :, :].rearrange("p k g s n -> p (k g s n)")
        wfg_f = xt_w[:, 0:128].rearrange("p (k n) -> p k n", k=KC)
        wh_f = xt_w[:, 128:640].rearrange("p (k n) -> p k n", k=KC)
        wqv_f = xt_w[:, 640:1152].rearrange("p (k n) -> p k n", k=KC)
        wk_f = xt_w[:, 1152:1408].rearrange("p (k n) -> p k n", k=KC)
        rows_f = xt_w[0:96, 1408:1408 + CODES]
        rows_r = xt_w[0:96, 2432:2432 + CODES]
        bfg_f = xt_w[0:96, 3456:3520]
        bo_f = xt_w[0:96, 3520:3776]
        wmean = xt_w[:, 3776:3778]
        wo_f = xt_w[:, 3800:4056]
        NW = 15

        @block.sync
        def _(sp):
            for dst, src in (
                (emb_f, emb.rearrange("(k p) n -> p k n", p=P)),
                (wfg_f, wfg.rearrange("(k p) n -> p k n", p=P)),
                (wh_f, wh.rearrange("(k p) n -> p k n", p=P)),
                (wqv_f, wqv.rearrange("(k p) n -> p k n", p=P)),
                (wk_f, wk.rearrange("(k p) n -> p k n", p=P)),
                (w3_sb[:, :, :], w3.rearrange("(k p) n -> p k n", p=P)),
                (wo_f, w_out),
                (h_bias[:, :], bh.partition_broadcast(P)),
                (b3_sb[:, :], b3.partition_broadcast(P)),
                (gamma_b[:, :], gamma.partition_broadcast(P)),
                (beta_c[:, :], beta),
                (bfg_f, bfg.partition_broadcast(96)),
                (bo_f, b_out.partition_broadcast(96)),
                (ident[:, :], ident_in),
                (gmat[:, :], gmat_in),
            ):
                sp.dma_start(dst, src).then_inc(weights_in, 16)
            for s in credited:
                sp.sem_inc(s.sem, s.depth)
            for s in range(2):
                sp.sem_inc(stored[s], 16)
            sp.sem_inc(start, 1)
            sp.wait_ge(start, 4)
            with sp.Fori(0, B) as im:
                for g in range(NG):
                    sp.wait_ge(a_turned.sem, a_turned.room(im * NG + g))
                    sp.dma_start(xin[:, g, :, :], xv[im, g]).then_inc(loaded[g], 16)

        @block.gpsimd
        def _(pool):
            pool.sem_inc(start, 1)
            pool.wait_ge(start, 4)
            with pool.Fori(0, B) as im:
                def gn(layer):
                    r = im * 4 + layer
                    pool.wait_ge(ve_ready.sem, ve_ready.after(r))
                    nc.gpsimd.tensor_tensor(gs[:, :], ve[:, :], mhalf2[:, 0:KC], ALU.pow).then_inc(pow_done.sem, 1)

                barrier(pool, im, 0)
                gn(0)

                def l0(at):
                    g = at(1)
                    if g is None:
                        return
                    for u in range(GT):
                        if u == 0:
                            pool.wait_ge(l0_turned.sem, l0_turned.room(g.n))
                        pool.wait_ge(l0_indexed.sem, l0_indexed.after(g.n * GT + u))
                        apart(pool)
                        nc.gpsimd.indirect_dma_start(
                            quant[:, g.slot, u, :], None, emb_t,
                            bass.IndirectOffsetOnAxis(ap=idx[:, g.slot * GT + u, 0:1], axis=0),
                        ).then_inc(gathered[g.slot][u], 16)

                pipeline(pool, im, 3, l0)
                barrier(pool, im, 1)
                gn(1)
                barrier(pool, im, 2)
                gn(2)
                barrier(pool, im, 3)
                barrier(pool, im, 4)

                def l2_add(at):
                    g = at(0)
                    if g is None:
                        return
                    pool.wait_ge(g_gated.sem, g_gated.after(g.n))
                    nc.gpsimd.tensor_tensor(XT[:, :, g.pair, g.slot, :], XT[:, :, g.pair, g.slot, :],
                                            gated[:, g.slot, :, :], ALU.add).then_inc(g_added.sem, 1)

                pipeline(pool, im, 1, l2_add)
                barrier(pool, im, 5)
                gn(3)
                barrier(pool, im, 6)
                barrier(pool, im, 7)

                def l3_pow(at):
                    g = at(1)
                    if g is None:
                        return
                    pool.wait_ge(f_ve.sem, f_ve.after(g.n))
                    nc.gpsimd.tensor_tensor(rstd[:, g.slot, 1, :], rstd[:, g.slot, 0, :], mhalf2[:, :],
                                            ALU.pow).then_inc(f_rstd.sem, 1)

                pipeline(pool, im, 2, l3_pow)
                barrier(pool, im, 8)

        @block.scalar
        def _(act):
            act.sem_inc(start, 1)
            act.wait_ge(start, 4)
            with act.Fori(0, B) as im:
                def norm(g, made, free, hi=None, hi_free=None):
                    act.wait_ge(*free)
                    for k in range(KC):
                        last = nc.scalar.activation(xn[:, g.slot, k, :], XT[:, k, g.pair, g.slot, :], ACT.Identity,
                                                    scale=gs[:, k:k + 1], bias=gt[:, k:k + 1])
                    last.then_inc(made.sem, 1)
                    if hi is not None:
                        act.wait_ge(*hi_free)
                        act.wait_ge(made.sem, made.after(g.n))
                        nc.scalar.activation(xhi[:, g.slot, :, :], xn[:, g.slot, :, :], ACT.Identity).then_inc(hi.sem, 1)

                for s in range(NG):
                    n = im * NG + s
                    b = 2 * (s % 2)
                    act.wait_ge(a_turned.sem, a_turned.after(n))
                    nc.scalar.activation(XT[:, :, s // 2, s % 2, :], PS[:, b:b + 2, :], ACT.Identity).then_inc(a_kept.sem, 1)
                barrier(act, im, 0)

                def l0(at):
                    g = at(0)
                    if g is not None:
                        norm(g, l0_xn, (l0_lo.sem, l0_lo.room(g.n)), l0_hi,
                             (l0_scored.sem, l0_scored.room(g.n * GT + GT - 1)))

                act.wait_ge(gn_ready.sem, gn_ready.after(im * 4))
                pipeline(act, im, 1, l0)
                barrier(act, im, 1)

                def l1(at):
                    g = at(0)
                    if g is not None:
                        norm(g, l1_xn, (l1_lo.sem, l1_lo.room(g.n)), l1_hi, (l1_h.sem, l1_h.room(g.n * 2 + 1)))
                    g = at(1)
                    if g is not None:
                        act.wait_ge(l1_fg.sem, l1_fg.after(g.n))
                        act.wait_ge(l1_scores.sem, l1_scores.room(g.n))
                        nc.scalar.activation(FT[:, g.slot, :], PS[0:CK, g.slot, :], ACT.Identity)
                        nc.scalar.activation(GTm[:, g.slot, :], PS[CK:2 * CK, g.slot, :],
                                             ACT.Identity).then_inc(l1_fgkept.sem, 1)
                        act.wait_ge(l1_scores.sem, l1_scores.after(g.n))
                        act.wait_ge(l1_out.sem, l1_out.room(g.n))
                        src = PS[:, 2 + g.slot, :].rearrange("p (u n) -> p u n", u=GT)
                        for r in range(P // ROW):
                            rr = slice(r * ROW, (r + 1) * ROW)
                            last = nc.scalar.activation(attn[rr, g.slot, :, rr], src[rr, :, rr], ACT.Sigmoid)
                        last.then_inc(l1_attn.sem, 1)

                act.wait_ge(gn_ready.sem, gn_ready.after(im * 4 + 1))
                pipeline(act, im, 2, l1)
                barrier(act, im, 2)

                def l2_norm(at):
                    g = at(0)
                    if g is not None:
                        norm(g, l2_xn, (l2_proj.sem, l2_proj.room(g.n)))

                act.wait_ge(gn_ready.sem, gn_ready.after(im * 4 + 2))
                pipeline(act, im, 1, l2_norm)
                for s in range(NG):
                    n = im * NG + s
                    act.wait_ge(pieces_turned.sem, pieces_turned.after(n))
                    nc.scalar.activation(lhs_p[:, s * GW:(s + 1) * GW], PS[0:PIECES, s % 2, :], ACT.Identity)
                    nc.scalar.activation(rhs_p[:, s * GW:(s + 1) * GW], PS[BROW:BROW + PIECES, s % 2, :],
                                         ACT.Identity).then_inc(pieces_kept.sem, 1)
                barrier(act, im, 3)

                def exps(i, j, tt):
                    for z in range(4):
                        c = (im * NT + i * TRIO + tt) * 4 + z
                        zone = (tt * 4 + z) % ZONES
                        e = (tt * 2 + z // 2) % TRIO
                        act.wait_ge(exps_in.sem, exps_in.after(c))
                        if z % 2 == 0:
                            act.wait_ge(sums_done.sem, sums_done.room((im * NT + i * TRIO + tt) * 2 + z // 2, TRIO))
                        nc.scalar.activation(E[:, e, (z % 2) * ZW:(z % 2 + 1) * ZW],
                                             PS[:, 2 * zone:2 * zone + 2, :].rearrange("p a n -> p (a n)"),
                                             ACT.Exp).then_inc(exps_done.sem, 1)

                with act.Fori(0, NT // TRIO) as i:
                    for tt in range(TRIO):
                        exps(i, tt, tt)
                for tt in range(NT - NT // TRIO * TRIO):
                    exps(NT // TRIO, tt, tt)
                act.wait_ge(sums_done.sem, sums_done.after((im + 1) * (NT * NHALF) - 1))
                nc.scalar.activation(accs, PS[:, 6:8, :].rearrange("p a n -> p (a n)"), ACT.Identity).then_inc(acc_kept.sem, 1)
                act.wait_ge(gate_made.sem, gate_made.after(im))
                nc.scalar.activation(gate[:, 1, :], gate[:, 0, :], ACT.Exp, scale=-1.0).then_inc(gate_exp.sem, 1)
                barrier(act, im, 4)

                def l2_gate(at):
                    g = at(0)
                    if g is not None:
                        norm(g, g_xn, (g_gated.sem, g_gated.room(g.n)))

                pipeline(act, im, 1, l2_gate)
                barrier(act, im, 5)

                def l3(at):
                    g = at(0)
                    if g is not None:
                        norm(g, l3_xn, (l3_lo.sem, l3_lo.room(g.n)), l3_hi, (l3_qv.sem, l3_qv.room(g.n)))
                    g = at(1)
                    if g is not None:
                        act.wait_ge(l3_k.sem, l3_k.after(g.n))
                        nc.scalar.activation(KTs[:, g.pair, g.slot, :], PS[:, g.slot, :], ACT.Identity).then_inc(l3_kkept.sem, 1)
                        act.wait_ge(l3_qv.sem, l3_qv.after(g.n))
                        nc.scalar.activation(V[:, g.pair, g.slot, :, :], qv_ps(g)[:, :, HID:2 * HID],
                                             ACT.Identity).then_inc(l3_vkept.sem, 1)
                        act.wait_ge(l3_qsub.sem, l3_qsub.after(g.n))
                        nc.scalar.activation(qe[:, g.slot, :, :], qe[:, g.slot, :, :], ACT.Exp).then_inc(l3_qexp.sem, 1)
                    g = at(2)
                    if g is not None:
                        act.wait_ge(l3_qt.sem, l3_qt.after(g.n))
                        nc.scalar.activation(q_hi[:, g.pair, g.slot, :, :],
                                             PS[:, 6 + g.slot, :].rearrange("p (u n) -> p u n", u=GT),
                                             ACT.Identity).then_inc(l3_qhi.sem, 1)

                act.wait_ge(gn_ready.sem, gn_ready.after(im * 4 + 3))
                pipeline(act, im, 3, l3)
                barrier(act, im, 6)

                def l3_keys(at):
                    g = at(0)
                    if g is not None:
                        act.wait_ge(l3_kturned.sem, l3_kturned.room(g.n))
                        nc.scalar.activation(ke[:, g.slot, :, :].rearrange("p u n -> p (u n)"),
                                             KTs[:, g.pair, g.slot, :], ACT.Exp, bias=kneg[:, :],
                                             accum_out=ksum[:, g.pair, g.slot:g.slot + 1]).then_inc(l3_kexp.sem, 1)

                act.wait_ge(kneg_ready.sem, kneg_ready.after(im))
                pipeline(act, im, 1, l3_keys)
                act.wait_ge(m_ps.sem, m_ps.after(im))
                act.wait_ge(ctxd_ready.sem, ctxd_ready.after(im))
                nc.scalar.activation(m_hi[:, :], PS[:, 5, 0:C], ACT.Identity).then_inc(mhi_ready.sem, 1)
                barrier(act, im, 7)

                def final(at):
                    g = at(0)
                    if g is not None:
                        act.wait_ge(f_turned.sem, f_turned.room(g.n))
                        for k in range(KC):
                            last = nc.scalar.activation(xb[:, g.slot, k, :], XT[:, k, g.pair, g.slot, :], ACT.Identity,
                                                        bias=beta_c[:, k:k + 1])
                        last.then_inc(f_xb.sem, 1)
                    g = at(1)
                    if g is not None:
                        act.wait_ge(f_z.sem, f_z.after(g.n))
                        act.wait_ge(f_y.sem, f_y.room(g.n))
                        for u in range(GT):
                            last = nc.scalar.activation(squares[:, g.slot, u, :], z_ps(g)[:, u, :], ACT.Square,
                                                        accum_out=sq[:, g.slot, u:u + 1])
                        last.then_inc(f_sq.sem, 1)
                    g = at(2)
                    if g is not None:
                        act.wait_ge(f_out.sem, f_out.after(g.n))
                        act.dma_start(ov[im, :, g.pair, g.slot, :, :], yout[:, g.slot, :, :]).then_inc(stored[g.slot], 16)

                pipeline(act, im, 3, final)
                barrier(act, im, 8)
            for s in range(2):
                act.wait_ge(stored[s], 16 + 16 * B * NG // 2)

        @block.vector
        def _(dve):
            v = nc.vector
            chain = [0]

            def link(ins):
                chain[0] += 1
                ins.then_inc(setup_dve, 1)
                dve.wait_ge(setup_dve, chain[0])

            def pieces(dst, src, rem, w):
                for j in range(3):
                    rr = slice(32 * j, 32 * j + 32)
                    link(v.tensor_copy(dst[rr, 0:w], src[rr, 0:w]))
                    if j < 2:
                        for q in range(j + 1, 3):
                            tail = slice(32 * q, 32 * q + 32)
                            link(v.tensor_copy(rem[tail, 0:w], dst[rr, 0:w]))
                            link(v.tensor_tensor(src[tail, 0:w], src[tail, 0:w], rem[tail, 0:w], ALU.subtract))

            for t, val in ((ones, 1.0), (minus_half, -0.5), (mhalf2, -0.5), (attn, 0.0), (w2, 0.0), (zero_w, 0.0),
                           (ctxd, 0.0), (onesel, 0.0)):
                link(v.memset(t[:], val))
            for j in range(3):
                link(v.memset(onesel[32 * j:32 * j + 1, :], 1.0))
            link(v.memset(w2[:, :, 1:2], 1.0))
            dve.wait_ge(weights_in, 16 * NW)
            for src, hi, lo in ((emb_f, e_hi, e_lo), (wfg_f, fg_hi, fg_lo), (wh_f, h_hi, h_lo), (wqv_f, qv_hi, qv_lo),
                                (wk_f, k_hi, k_lo)):
                link(v.tensor_copy(hi[:], src))
                link(v.tensor_tensor(lo[:], src, hi[:], ALU.subtract))
            v.tensor_tensor(emb_q, emb_f, emb_f, ALU.mult).then_inc(emb_squared, 1)
            dve.wait_ge(setup_pe, 1)
            link(v.tensor_copy(rows_f, PS[0:96, 0:2, :].rearrange("p a n -> p (a n)")))
            pieces(e_bias, rows_f, rows_r, CODES)
            pieces(fg_bias, bfg_f, rows_r, 2 * CK)
            link(v.tensor_reduce(wmean[:, 0:1], wo_f, AX, ALU.add))
            link(v.tensor_scalar(wmean[:, 1:2], wmean[:, 0:1], 1.0 / C, None, ALU.mult))
            link(v.tensor_scalar(wo_c[:, :], wo_f, wmean[:, 1:2], None, ALU.subtract))
            link(v.tensor_reduce(wmean[0:96, 0:1], bo_f, AX, ALU.add))
            link(v.tensor_scalar(wmean[0:96, 1:2], wmean[0:96, 0:1], 1.0 / C, None, ALU.mult))
            link(v.tensor_scalar(bo_f, bo_f, wmean[0:96, 1:2], KAPPA, ALU.subtract, ALU.mult))
            pieces(z_bias, bo_f, rows_r, C)
            dve.sem_inc(start, 1)
            dve.wait_ge(start, 4)

            with dve.Fori(0, B) as im:
                def gn(layer, stat):
                    r = im * 4 + layer
                    gn_chain.start(r)
                    dve.wait_ge(stat.sem, stat.after(im * NG + NG - 1))
                    for k in range(KC):
                        apart(dve)
                        gn_chain.link(dve, v.bn_aggr(mv[:, k, :], stats[:, k, :, :, :].rearrange("p g s n -> p (g s n)")))
                    v.tensor_copy(dm[:, :], mv[:, :, 0]).then_inc(mean_ready.sem, 1)
                    dve.wait_ge(mean_ps.sem, mean_ps.after(r))
                    dve.wait_ge(mean_ready.sem, mean_ready.after(r))
                    v.tensor_copy(gm[:, :], PS[:, 7, 0:KC])
                    gn_chain.link(dve, v.tensor_tensor(dm[:, :], dm[:, :], PS[:, 7, 0:KC], ALU.subtract))
                    gn_chain.link(dve, v.tensor_tensor(vv[:, :], dm[:, :], dm[:, :], ALU.mult))
                    v.tensor_tensor(vv[:, :], vv[:, :], mv[:, :, 1], ALU.add).then_inc(var_ready.sem, 1)
                    dve.wait_ge(var_ps.sem, var_ps.after(r))
                    v.tensor_scalar(ve[:, :], PS[:, 7, 4:4 + KC], GN_EPS, None, ALU.add).then_inc(ve_ready.sem, 1)
                    dve.wait_ge(pow_done.sem, pow_done.after(r))
                    v.scalar_tensor_tensor(out=gt[:, :], in0=gm[:, :], scalar=-1.0, in1=gs[:, :], op0=ALU.mult,
                                           op1=ALU.mult).then_inc(gn_ready.sem, 1)
                    gn_chain.end()

                def low(g, hi, lo, free):
                    dve.wait_ge(hi.sem, hi.after(g.n))
                    dve.wait_ge(*free)
                    v.tensor_tensor(xlo[:, g.slot, :, :], xn[:, g.slot, :, :], xhi[:, g.slot, :, :],
                                    ALU.subtract).then_inc(lo.sem, 1)

                def stat(g, done):
                    for k in range(KC):
                        last = v.bn_stats(stats[:, k, g.pair, g.slot, :], XT[:, k, g.pair, g.slot, :])
                    last.then_inc(done.sem, 1)

                for s in range(NG):
                    g = Group(im, 0, s)
                    dve.wait_ge(a_kept.sem, a_kept.after(g.n))
                    stat(g, stats_done[0])
                barrier(dve, im, 0)
                gn(0, stats_done[0])

                def l0(at):
                    g = at(0)
                    if g is not None:
                        low(g, l0_hi, l0_lo, (l0_scored.sem, l0_scored.room(g.n * GT + GT - 1)))
                    g, add = at(1), at(2)
                    if g is not None:
                        for u in range(GT):
                            t = g.n * GT + u
                            b = 2 * (u % 2)
                            scores = PS[:, b:b + 2, :].rearrange("p a n -> p (a n)")
                            dve.wait_ge(l0_scored.sem, l0_scored.after(t))
                            apart(dve)
                            v.max(m8[:, u % 2, :], scores).then_inc(l0_maxed.sem, 1)
                            dve.wait_ge(l0_maxed.sem, l0_maxed.after(t))
                            apart(dve)
                            v.max_index(idx[:, g.slot * GT + u, :], m8[:, u % 2, :], scores).then_inc(l0_indexed.sem, 1)
                    if add is not None:
                        dve.wait_ge(l0_turned.sem, l0_turned.after(add.n))
                        here = XT[:, :, add.pair, add.slot, :]
                        v.tensor_tensor(here, here, PS[:, 4 + 2 * add.slot:6 + 2 * add.slot, :],
                                        ALU.add).then_inc(l0_added.sem, 1)
                        dve.wait_ge(l0_added.sem, l0_added.after(add.n))
                        stat(add, stats_done[1])

                pipeline(dve, im, 3, l0)
                barrier(dve, im, 1)
                gn(1, stats_done[1])

                def l1(at):
                    g = at(0)
                    if g is not None:
                        low(g, l1_hi, l1_lo, (l1_h.sem, l1_h.room(g.n * 2 + 1)))
                    g = at(1)
                    if g is not None:
                        dve.wait_ge(l1_out.sem, l1_out.room(g.n))
                        for w in range(2):
                            dve.wait_ge(l1_h.sem, l1_h.after(g.n * 2 + w))
                            v.tensor_tensor(H[:, g.slot, 2 * w:2 * w + 2, :],
                                            PS[:, 4 + w, :].rearrange("p (u n) -> p u n", u=2),
                                            h_bias[:, :].unsqueeze(1).broadcast_to([P, 2, C]),
                                            ALU.add).then_inc(l1_hkept.sem, 1)
                    g = at(2)
                    if g is not None:
                        dve.wait_ge(l1_out.sem, l1_out.after(g.n))
                        here = XT[:, :, g.pair, g.slot, :]
                        v.tensor_tensor(here, here, PS[:, 6:8, :], ALU.add).then_inc(l1_added.sem, 1)
                        dve.wait_ge(l1_added.sem, l1_added.after(g.n))
                        stat(g, stats_done[2])

                pipeline(dve, im, 3, l1)
                barrier(dve, im, 2)
                gn(2, stats_done[2])

                small_chain.start(im)
                sc = small_chain
                dve.wait_ge(l2_proj.sem, l2_proj.after(im * NG + NG - 1))
                proj = PS[:, 6, 0:4 * NT].rearrange("p (t k) -> p k t", k=4)
                v.tensor_scalar(x2c[:, :], proj[:, 2, :], b3_sb[:, 2:3], None, ALU.add)
                v.tensor_scalar(s3[:, 0, :], proj[:, 0, :], b3_sb[:, 0:1], None, ALU.add)
                sc.link(dve, v.tensor_scalar(s3[:, 1, :], proj[:, 1, :], b3_sb[:, 1:2], None, ALU.add))
                v.tensor_reduce(mm2[:, 0:1], s3[:, 0, :], AX, ALU.max)
                v.tensor_reduce(mm2[:, 1:2], s3[:, 0, :], AX, ALU.min, negate=True).then_inc(x0max_in.sem, 1)
                dve.wait_ge(x0max_t.sem, x0max_t.after(im))
                sc.link(dve, v.tensor_reduce(mt2[:, :], PS[0:2, 0, 0:P], AX, ALU.max))
                v.tensor_scalar(dg2[:, :], ident[0:2, 0:2], mt2[:, 0:1], None, ALU.mult).then_inc(x0max_d.sem, 1)
                dve.wait_ge(x0max_b.sem, x0max_b.after(im))
                sc.link(dve, v.tensor_copy(mx2[:, :], PS[:, 1, 0:2]))
                v.tensor_scalar(ma[:, 0, :], s3[:, 1, :], mx2[:, 0:1], None, ALU.mult)
                sc.link(dve, v.tensor_scalar(ma[:, 1, :], s3[:, 1, :], mx2[:, 1:2], -1.0, ALU.mult, ALU.mult))
                sc.link(dve, v.tensor_tensor(s3[:, 2, :], ma[:, 0, :], ma[:, 1, :], ALU.max))
                sc.link(dve, v.tensor_copy(pk[:, 0, :, :], s3[:, :, :]))
                sc.link(dve, v.tensor_tensor(r3[:, 0, :, :], s3[:, :, :], pk[:, 0, :, :], ALU.subtract))
                sc.link(dve, v.tensor_copy(pk[:, 1, :, :], r3[:, 0, :, :]))
                sc.link(dve, v.tensor_tensor(r3[:, 1, :, :], r3[:, 0, :, :], pk[:, 1, :, :], ALU.subtract))
                sc.link(dve, v.tensor_copy(pk[:, 2, :, :], r3[:, 1, :, :]))
                v.memset(pc[:, :, PIECES:BROW], 0.0)
                v.memset(pc[:, :, 9:PIECES], -1.0)
                for j in range(3):
                    v.tensor_copy(pc[:, :, 3 * j:3 * j + 3],
                                  pk[:, j, 0, :].unsqueeze(2).broadcast_to([P, NT, 3]))
                    v.tensor_copy(pc[:, :, BROW + j:BROW + 9:3],
                                  pk[:, j, 1, :].unsqueeze(2).broadcast_to([P, NT, 3]))
                    last = v.tensor_copy(pc[:, :, BROW + 9 + j], pk[:, j, 2, :])
                last.then_inc(pieces_made.sem, 1)
                sc.end()
                barrier(dve, im, 3)

                body = NT // TRIO
                lhs_tiles = lhs_p[:, 0:body * TRIO * P].rearrange("p (i t n) -> p i t n", t=TRIO, n=P)
                x2_trio = x2c[:, 0:body * TRIO].rearrange("p (i t) -> p i t", t=TRIO)
                with dve.Fori(0, body) as i:
                    for tt in range(TRIO):
                        dve.wait_ge(sums_done.sem, sums_done.room((im * NT + i * TRIO + tt) * 2 + 1))
                        v.tensor_copy(lhs_s[:, tt, :], lhs_tiles[:, i, tt, :])
                        v.tensor_copy(w2[:, tt, 0:1], x2_trio[:, i, tt:tt + 1]).then_inc(tile_staged.sem, 1)
                for tt in range(NT - body * TRIO):
                    dve.wait_ge(sums_done.sem, sums_done.room((im * NT + body * TRIO + tt) * 2 + 1))
                    t = body * TRIO + tt
                    v.tensor_copy(lhs_s[:, tt, :], lhs_p[:, t * P:(t + 1) * P])
                    v.tensor_copy(w2[:, tt, 0:1], x2c[:, t:t + 1]).then_inc(tile_staged.sem, 1)

                gate_chain.start(im)
                gc = gate_chain
                dve.wait_ge(acc_turned.sem, acc_turned.after(im))
                at_ps = PS[:, 0:NHALF, :].rearrange("p f (j q r) -> p f q j r", j=GT, q=QUADS)
                gview = gate[:, :, :].rearrange("p a (f q j) -> p a f q j", f=NHALF, q=QUADS)
                for f in range(NHALF):
                    last = v.tensor_copy(nums[:, f, :, :], at_ps[:, f, :, :, 1])
                gc.link(dve, last)
                gc.link(dve, v.reciprocal(nums[:, :, :, :], nums[:, :, :, :]))
                for f in range(NHALF):
                    last = v.tensor_tensor(gview[:, 0, f, :, :], at_ps[:, f, :, :, 0], nums[:, f, :, :], ALU.mult)
                last.then_inc(gate_made.sem, 1)
                dve.wait_ge(gate_exp.sem, gate_exp.after(im))
                gc.link(dve, v.tensor_scalar(gate[:, 1, :], gate[:, 1, :], 1.0, None, ALU.add))
                gc.link(dve, v.reciprocal(gate[:, 2, :], gate[:, 1, :]))
                gc.end()
                barrier(dve, im, 4)

                def l2_gate(at):
                    g = at(0)
                    if g is not None:
                        gcol = gate[:, 2, :].rearrange("p (q s u) -> p q s u", q=NG // 2, s=2)
                        dve.wait_ge(g_spread.sem, g_spread.room(g.n))
                        v.tensor_tensor(diag[:, g.slot, :, :],
                                        ident[:, :].unsqueeze(1).broadcast_to([P, GT, P]),
                                        gcol[:, g.pair, g.slot, :].unsqueeze(2).broadcast_to([P, GT, P]),
                                        ALU.mult).then_inc(g_diag.sem, 1)
                    g = at(1)
                    if g is not None:
                        dve.wait_ge(g_xn.sem, g_xn.after(g.n))
                        dve.wait_ge(g_spread.sem, g_spread.after(g.n))
                        dve.wait_ge(g_added.sem, g_added.room(g.n))
                        v.tensor_tensor(gated[:, g.slot, :, :], xn[:, g.slot, :, :],
                                        PS[:, g.slot, :].unsqueeze(1).broadcast_to([P, KC, GW]),
                                        ALU.mult).then_inc(g_gated.sem, 1)
                    g = at(2)
                    if g is not None:
                        dve.wait_ge(g_added.sem, g_added.after(g.n))
                        stat(g, stats_done[3])

                pipeline(dve, im, 3, l2_gate)
                barrier(dve, im, 5)
                gn(3, stats_done[3])

                def l3(at):
                    g = at(0)
                    if g is not None:
                        low(g, l3_hi, l3_lo, (l3_qv.sem, l3_qv.room(g.n)))
                    g = at(1)
                    if g is not None:
                        dve.wait_ge(l3_kkept.sem, l3_kkept.after(g.n))
                        v.tensor_reduce(kmx[:, g.pair, g.slot:g.slot + 1], KTs[:, g.pair, g.slot, :], AX,
                                        ALU.max).then_inc(l3_kmax.sem, 1)
                        dve.wait_ge(l3_vkept.sem, l3_vkept.after(g.n))
                        q_ps = qv_ps(g)[:, :, 0:HID]
                        q_chain.start(g.n)
                        qm = qmx[:, g.slot, :].rearrange("p (u h) -> p u h", u=GT)
                        for u in range(GT):
                            last = v.tensor_reduce(qm[:, u, :], q_ps[:, u, :].rearrange("p (h d) -> p h d", h=HEADS),
                                                   AX, ALU.max)
                        q_chain.link(dve, last)
                        for u in range(GT):
                            last = v.tensor_tensor(
                                qe[:, g.slot, u, :].rearrange("p (h d) -> p h d", h=HEADS),
                                q_ps[:, u, :].rearrange("p (h d) -> p h d", h=HEADS),
                                qm[:, u, :].unsqueeze(2).broadcast_to([P, HEADS, DH]), ALU.subtract)
                        last.then_inc(l3_qsub.sem, 1)
                        dve.wait_ge(l3_qexp.sem, l3_qexp.after(g.n))
                        flat = qe[:, g.slot, :, :].rearrange("p u (h d) -> p (u h) d", h=HEADS)
                        q_chain.link(dve, v.tensor_reduce(qsum[:, g.slot, 0, :], flat, AX, ALU.add))
                        q_chain.link(dve, v.reciprocal(qsum[:, g.slot, 1, :], qsum[:, g.slot, 0, :]))
                        q_chain.end()
                        dve.wait_ge(l3_qt.sem, l3_qt.room(g.n))
                        v.tensor_tensor(qs[:, g.slot, :, :].rearrange("p u (h d) -> p (u h) d", h=HEADS), flat,
                                        qsum[:, g.slot, 1, :].unsqueeze(2).broadcast_to([P, GT * HEADS, DH]),
                                        ALU.mult).then_inc(l3_qsoft.sem, 1)
                    g = at(2)
                    if g is not None:
                        dve.wait_ge(l3_qhi.sem, l3_qhi.after(g.n))
                        v.tensor_tensor(q_lo[:, g.pair, g.slot, :, :],
                                        PS[:, 6 + g.slot, :].rearrange("p (u n) -> p u n", u=GT),
                                        q_hi[:, g.pair, g.slot, :, :], ALU.subtract).then_inc(l3_qlo.sem, 1)

                pipeline(dve, im, 3, l3)
                k_chain.start(im)
                kc_ = k_chain
                dve.wait_ge(l3_kmax.sem, l3_kmax.after(im * NG + NG - 1))
                v.tensor_reduce(kneg[:, :], kmx[:, :, :].rearrange("p g s -> p (g s)"), AX, ALU.max,
                                negate=True).then_inc(kneg_ready.sem, 1)
                barrier(dve, im, 6)

                def l3_keys(at):
                    g = at(0)
                    if g is not None:
                        dve.wait_ge(l3_kturned.sem, l3_kturned.after(g.n))
                        dve.wait_ge(l3_ctx.sem, l3_ctx.room(g.n))
                        v.tensor_copy(kt[:, g.slot, :, :],
                                      PS[:, g.slot, :].rearrange("p (u n) -> p u n", u=GT)).then_inc(l3_kback.sem, 1)

                pipeline(dve, im, 1, l3_keys)
                dve.wait_ge(ctx_done.sem, ctx_done.after(im))
                dve.wait_ge(l3_kexp.sem, l3_kexp.after(im * NG + NG - 1))
                kc_.link(dve, v.tensor_reduce(kden[:, 0:1], ksum[:, :, :].rearrange("p g s -> p (g s)"), AX, ALU.add))
                kc_.link(dve, v.reciprocal(kden[:, 1:2], kden[:, 0:1]))
                kc_.link(dve, v.tensor_scalar(kden[:, 0:1], kden[:, 1:2], KAPPA * DH ** -0.5, None, ALU.mult))
                for h in range(HEADS):
                    hh = slice(h * DH, (h + 1) * DH)
                    last = v.tensor_scalar(ctxd[hh, hh], PS[hh, 4, hh], kden[hh, 0:1], None, ALU.mult)
                last.then_inc(ctxd_ready.sem, 1)
                dve.wait_ge(ctxt_ps.sem, ctxt_ps.after(im))
                v.tensor_copy(ctxt[:, :], PS[:, 6, 0:P]).then_inc(ctxt_ready.sem, 1)
                dve.wait_ge(mhi_ready.sem, mhi_ready.after(im))
                v.tensor_tensor(m_lo[:, :], PS[:, 5, 0:C], m_hi[:, :], ALU.subtract).then_inc(mlo_ready.sem, 1)
                kc_.end()
                barrier(dve, im, 7)

                def final(at):
                    g = at(1)
                    if g is not None:
                        dve.wait_ge(f_sq.sem, f_sq.after(g.n))
                        v.tensor_scalar(rstd[:, g.slot, 0, :], sq[:, g.slot, :], 1.0 / C, LN_EPS * KAPPA * KAPPA,
                                        ALU.mult, ALU.add).then_inc(f_ve.sem, 1)
                        dve.wait_ge(f_rstd.sem, f_rstd.after(g.n))
                        for u in range(GT):
                            last = v.scalar_tensor_tensor(out=Y[:, g.slot, u, :], in0=z_ps(g)[:, u, :],
                                                          scalar=rstd[:, g.slot, 1, u:u + 1], in1=gamma_b[:, :],
                                                          op0=ALU.mult, op1=ALU.mult)
                        last.then_inc(f_y.sem, 1)
                        dve.wait_ge(f_y.sem, f_y.after(g.n))
                        dve.wait_ge(f_turned.sem, f_turned.after(g.n))
                        dve.wait_ge(stored[g.slot], 16 * (g.occ + 1))
                        v.tensor_tensor(yout[:, g.slot, :, :], Y[:, g.slot, :, :], xt_ps(g),
                                        ALU.add).then_inc(f_out.sem, 1)

                pipeline(dve, im, 2, final)
                barrier(dve, im, 8)

        @block.tensor
        def _(pe):
            mm, tr = nc.tensor.matmul, nc.tensor.transpose

            def split(dst, l_hi, l_lo, r_hi, r_lo, first, last):
                for j, (a, b) in enumerate(((l_hi, r_hi), (l_hi, r_lo), (l_lo, r_hi))):
                    ins = mm(dst, a, b, start=first and j == 0, stop=last and j == 2)
                return ins

            pe.wait_ge(emb_squared, 1)
            for b in range(2):
                for k in range(KC):
                    ins = mm(PS[0:96, b, :], minus_half[:, :], emb_q[:, k, b * 512:(b + 1) * 512],
                             start=k == 0, stop=k == KC - 1)
            ins.then_inc(setup_pe, 1)
            pe.wait_ge(start, 4)

            with pe.Fori(0, B) as im:
                def gn(layer):
                    r = im * 4 + layer
                    pe.wait_ge(mean_ready.sem, mean_ready.after(r))
                    mm(PS[:, 7, 0:KC], gmat[:, :], dm[:, :], start=True, stop=True).then_inc(mean_ps.sem, 1)
                    pe.wait_ge(var_ready.sem, var_ready.after(r))
                    mm(PS[:, 7, 4:4 + KC], gmat[:, :], vv[:, :], start=True, stop=True).then_inc(var_ps.sem, 1)

                for s in range(NG):
                    n = im * NG + s
                    b = 2 * (s % 2)
                    pe.wait_ge(loaded[s], (im + 1) * 16)
                    pe.wait_ge(a_kept.sem, a_kept.room(n))
                    for u in range(GT):
                        for k in range(KC):
                            ins = tr(PS[:, b + k, u * P:(u + 1) * P], xin[:, s, u, k * P:(k + 1) * P], ident[:, :])
                    ins.then_inc(a_turned.sem, 1)
                barrier(pe, im, 0)
                gn(0)

                def l0(at):
                    g, old = at(1), at(2)
                    for u in range(GT):
                        if g is not None:
                            if u == 0:
                                pe.wait_ge(l0_lo.sem, l0_lo.after(g.n))
                            t = g.n * GT + u
                            cols = slice(u * P, (u + 1) * P)
                            pe.wait_ge(l0_indexed.sem, l0_indexed.room(t))
                            for b in range(2):
                                dst = PS[:, 2 * (u % 2) + b, :]
                                half = slice(b * 512, (b + 1) * 512)
                                mm(dst, onesel[:, 0:P], e_bias[:, half], start=True, stop=False)
                                for k in range(KC):
                                    ins = split(dst, xhi[:, g.slot, k, cols], xlo[:, g.slot, k, cols],
                                                e_hi[:, k, half], e_lo[:, k, half], False, k == KC - 1)
                            ins.then_inc(l0_scored.sem, 1)
                        if old is not None:
                            if u == 0:
                                pe.wait_ge(l0_added.sem, l0_added.room(old.n))
                            pe.wait_ge(gathered[old.slot][u], (old.occ + 1) * 16)
                            for k in range(KC):
                                ins = tr(PS[:, 4 + 2 * old.slot + k, u * P:(u + 1) * P],
                                         quant[:, old.slot, u, k * P:(k + 1) * P], ident[:, :])
                            if u == GT - 1:
                                ins.then_inc(l0_turned.sem, 1)

                pipeline(pe, im, 3, l0)
                barrier(pe, im, 1)
                gn(1)

                def l1(at):
                    g = at(1)
                    if g is not None:
                        pe.wait_ge(l1_lo.sem, l1_lo.after(g.n))
                        pe.wait_ge(l1_fgkept.sem, l1_fgkept.room(g.n))
                        dst = PS[0:2 * CK, g.slot, :]
                        mm(dst, fg_bias[:, :], onesel[:, :], start=True, stop=False)
                        for k in range(KC):
                            ins = split(dst, fg_hi[:, k, :], fg_lo[:, k, :], xhi[:, g.slot, k, :], xlo[:, g.slot, k, :],
                                        False, k == KC - 1)
                        ins.then_inc(l1_fg.sem, 1)
                        for w in range(2):
                            pe.wait_ge(l1_hkept.sem, l1_hkept.room(g.n * 2 + w))
                            for u in range(2):
                                cols = slice((2 * w + u) * P, (2 * w + u + 1) * P)
                                for k in range(KC):
                                    ins = split(PS[:, 4 + w, u * C:(u + 1) * C], xhi[:, g.slot, k, cols],
                                                xlo[:, g.slot, k, cols], h_hi[:, k, :], h_lo[:, k, :],
                                                k == 0, k == KC - 1)
                            ins.then_inc(l1_h.sem, 1)
                        pe.wait_ge(l1_fgkept.sem, l1_fgkept.after(g.n))
                        pe.wait_ge(l1_attn.sem, l1_attn.room(g.n))
                        for u in range(GT):
                            cols = slice(u * P, (u + 1) * P)
                            ins = mm(PS[:, 2 + g.slot, cols], GTm[:, g.slot, cols], FT[:, g.slot, cols],
                                     start=True, stop=True)
                        ins.then_inc(l1_scores.sem, 1)
                    g = at(2)
                    if g is not None:
                        pe.wait_ge(l1_attn.sem, l1_attn.after(g.n))
                        pe.wait_ge(l1_hkept.sem, l1_hkept.after(g.n * 2 + 1))
                        pe.wait_ge(l1_added.sem, l1_added.room(g.n))
                        for k in range(KC):
                            for u in range(GT):
                                ins = mm(PS[:, 6 + k, u * P:(u + 1) * P], H[:, g.slot, u, k * P:(k + 1) * P],
                                         attn[:, g.slot, u, :], start=True, stop=True)
                        ins.then_inc(l1_out.sem, 1)

                pipeline(pe, im, 3, l1)
                barrier(pe, im, 2)
                gn(2)

                proj = PS[:, 6, 0:4 * NT].rearrange("p (g s u k) -> p g s u k", g=NG // 2, s=2, u=GT)

                def l2_proj_step(at):
                    g = at(0)
                    if g is not None:
                        pe.wait_ge(l2_xn.sem, l2_xn.after(g.n))
                        for u in range(GT):
                            for k in range(KC):
                                ins = mm(proj[:, g.pair, g.slot, u, 0:3], xn[:, g.slot, k, u * P:(u + 1) * P],
                                         w3_sb[:, k, :], start=k == 0, stop=k == KC - 1)
                        ins.then_inc(l2_proj.sem, 1)

                pipeline(pe, im, 1, l2_proj_step)
                pe.wait_ge(x0max_in.sem, x0max_in.after(im))
                tr(PS[0:2, 0, 0:P], mm2[:, :], ident[:, :]).then_inc(x0max_t.sem, 1)
                pe.wait_ge(x0max_d.sem, x0max_d.after(im))
                mm(PS[:, 1, 0:2], ones[0:2, :], dg2[:, :], start=True, stop=True).then_inc(x0max_b.sem, 1)
                pe.wait_ge(pieces_made.sem, pieces_made.after(im))
                for s in range(NG):
                    n = im * NG + s
                    pe.wait_ge(pieces_kept.sem, pieces_kept.room(n))
                    apart(pe)
                    for u in range(GT):
                        ins = tr(PS[0:44, s % 2, u * P:(u + 1) * P], pc[:, s * GT + u, :], ident[:, :])
                    ins.then_inc(pieces_turned.sem, 1)
                barrier(pe, im, 3)

                for f in range(NHALF):
                    for q in range(QUADS):
                        mm(PS[32 * q:32 * q + 32, 6 + f, :], zero_w[:, 0:32], xn[:, 0, 0, :], start=True, stop=False,
                           skip_group_check=True)

                def fill(i, tt, z):
                    c = (im * NT + i * TRIO + tt) * 4 + z
                    zone = (tt * 4 + z) % ZONES
                    if z == 0:
                        pe.wait_ge(tile_staged.sem, tile_staged.after(im * NT + i * TRIO + tt))
                    pe.wait_ge(exps_done.sem, exps_done.room(c))
                    for b in range(2):
                        m0 = z * ZW + b * 512
                        ins = mm(PS[:, 2 * zone + b, :], lhs_s[:, tt % TRIO, :], rhs_p[:, m0:m0 + 512],
                                 start=True, stop=True)
                    ins.then_inc(exps_in.sem, 1)

                def sums(i, tt, f, close=False):
                    t = im * NT + i * TRIO + tt
                    e = (tt * 2 + f) % TRIO
                    pe.wait_ge(exps_done.sem, exps_done.after(t * 4 + 2 * f + 1))
                    for q in range(QUADS):
                        ins = mm(PS[32 * q:32 * q + 32, 6 + f, :], w2[:, tt % TRIO, :], E[:, e, q * 512:(q + 1) * 512],
                                 start=False, stop=close, skip_group_check=True)
                    ins.then_inc(sums_done.sem, 1)

                body = NT // TRIO
                rest = NT - body * TRIO
                fill(0, 0, 0)
                fill(0, 0, 1)

                def half_step(i, tt, f, nxt, close=False):
                    if nxt is not None:
                        fill(*nxt)
                        fill(nxt[0], nxt[1], nxt[2] + 1)
                    sums(i, tt, f, close)

                with pe.Fori(0, body) as i:
                    for tt in range(TRIO):
                        half_step(i, tt, 0, (i, tt, 2))
                        half_step(i, tt, 1, (i, tt + 1, 0))
                for tt in range(rest):
                    half_step(body, tt, 0, (body, tt, 2), tt == rest - 1)
                    half_step(body, tt, 1, (body, tt + 1, 0) if tt < rest - 1 else None, tt == rest - 1)
                pe.wait_ge(acc_kept.sem, acc_kept.after(im))
                for f in range(NHALF):
                    for j in range(GT):
                        ins = tr(PS[:, f, j * P:(j + 1) * P], accs[:, f * 512 + j * P:f * 512 + (j + 1) * P], ident[:, :])
                ins.then_inc(acc_turned.sem, 1)
                barrier(pe, im, 4)

                def l2_spread(at):
                    g = at(0)
                    if g is not None:
                        pe.wait_ge(g_diag.sem, g_diag.after(g.n))
                        pe.wait_ge(g_gated.sem, g_gated.room(g.n))
                        mm(PS[:, g.slot, :], ones[:, :], diag[:, g.slot, :, :].rearrange("p u n -> p (u n)"),
                           start=True, stop=True).then_inc(g_spread.sem, 1)

                pipeline(pe, im, 1, l2_spread)
                barrier(pe, im, 5)
                gn(3)

                def l3(at):
                    g = at(1)
                    if g is not None:
                        pe.wait_ge(l3_lo.sem, l3_lo.after(g.n))
                        pe.wait_ge(l3_kkept.sem, l3_kkept.room(g.n))
                        for k in range(KC):
                            ins = split(PS[:, g.slot, :], k_hi[:, k, :], k_lo[:, k, :], xhi[:, g.slot, k, :],
                                        xlo[:, g.slot, k, :], k == 0, k == KC - 1)
                        ins.then_inc(l3_k.sem, 1)
                        pe.wait_ge(l3_vkept.sem, l3_vkept.room(g.n))
                        pe.wait_ge(l3_qsub.sem, l3_qsub.room(g.n))
                        for u in range(GT):
                            cols = slice(u * P, (u + 1) * P)
                            for k in range(KC):
                                ins = split(qv_ps(g)[:, u, :], xhi[:, g.slot, k, cols], xlo[:, g.slot, k, cols],
                                            qv_hi[:, k, :], qv_lo[:, k, :], k == 0, k == KC - 1)
                        ins.then_inc(l3_qv.sem, 1)
                    g = at(2)
                    if g is not None:
                        pe.wait_ge(l3_qsoft.sem, l3_qsoft.after(g.n))
                        pe.wait_ge(l3_qlo.sem, l3_qlo.room(g.n))
                        for u in range(GT):
                            ins = tr(PS[:, 6 + g.slot, u * P:(u + 1) * P], qs[:, g.slot, u, :], ident[:, :])
                        ins.then_inc(l3_qt.sem, 1)

                pipeline(pe, im, 3, l3)
                barrier(pe, im, 6)

                mm(PS[:, 4, 0:P], zero_w[:, :], ident[:, :], start=True, stop=False, skip_group_check=True)

                def l3_keys(at):
                    g = at(0)
                    if g is not None:
                        pe.wait_ge(l3_kexp.sem, l3_kexp.after(g.n))
                        pe.wait_ge(l3_kback.sem, l3_kback.room(g.n))
                        for u in range(GT):
                            ins = tr(PS[:, g.slot, u * P:(u + 1) * P], ke[:, g.slot, u, :], ident[:, :])
                        ins.then_inc(l3_kturned.sem, 1)
                    g = at(1)
                    if g is not None:
                        pe.wait_ge(l3_kback.sem, l3_kback.after(g.n))
                        for u in range(GT):
                            ins = mm(PS[:, 4, 0:P], kt[:, g.slot, u, :], V[:, g.pair, g.slot, u, :],
                                     start=False, stop=False, skip_group_check=True)
                        ins.then_inc(l3_ctx.sem, 1)

                pipeline(pe, im, 2, l3_keys)
                mm(PS[:, 4, 0:P], zero_w[:, :], ident[:, :], start=False, stop=True,
                   skip_group_check=True).then_inc(ctx_done.sem, 1)
                pe.wait_ge(ctxd_ready.sem, ctxd_ready.after(im))
                tr(PS[:, 6, 0:P], ctxd[:, :], ident[:, :]).then_inc(ctxt_ps.sem, 1)
                pe.wait_ge(ctxt_ready.sem, ctxt_ready.after(im))
                mm(PS[:, 5, 0:C], ctxt[:, :], wo_c[:, :], start=True, stop=True).then_inc(m_ps.sem, 1)
                barrier(pe, im, 7)

                def final(at):
                    g = at(1)
                    if g is not None:
                        pe.wait_ge(f_y.sem, f_y.room(g.n))
                        for u in range(GT):
                            dst = z_ps(g)[:, u, :]
                            mm(dst, onesel[:, 0:P], z_bias[:, :], start=True, stop=False)
                            ins = split(dst, q_hi[:, g.pair, g.slot, u, :], q_lo[:, g.pair, g.slot, u, :],
                                        m_hi[:, :], m_lo[:, :], False, True)
                        ins.then_inc(f_z.sem, 1)
                        pe.wait_ge(f_xb.sem, f_xb.after(g.n))
                        pe.wait_ge(f_out.sem, f_out.room(g.n))
                        for u in range(GT):
                            for k in range(KC):
                                ins = tr(xt_ps(g)[:, u, k * P:(k + 1) * P], xb[:, g.slot, k, u * P:(u + 1) * P],
                                         ident[:, :])
                        ins.then_inc(f_turned.sem, 1)

                pipeline(pe, im, 2, final)
                barrier(pe, im, 8)


def kernel(x, L0_conv_embeddings, L1_conv_Wf, L1_conv_bf, L1_conv_Wg, L1_conv_bg, L1_conv_Wh, L1_conv_bh,
           L2_conv_w1, L2_conv_b1, L2_conv_w2, L2_conv_b2, L2_conv_w3, L2_conv_b3,
           L3_conv_w_qkv, L3_conv_w_out, L3_conv_b_out, L3_conv_gamma, L3_conv_beta):
    import numpy as np
    import concourse.bacc as bacc
    from concourse.bass_utils import run_bass_kernel_spmd

    emb = np.asarray(L0_conv_embeddings)
    qkv = np.asarray(L3_conv_w_qkv)
    arrays = dict(
        x=np.asarray(x),
        emb=emb,
        emb_t=emb.T,
        wfg=np.concatenate([np.asarray(L1_conv_Wf), np.asarray(L1_conv_Wg)], axis=1),
        bfg=np.concatenate([np.asarray(L1_conv_bf), np.asarray(L1_conv_bg)]),
        wh=np.asarray(L1_conv_Wh),
        bh=np.asarray(L1_conv_bh),
        w3=np.stack([np.asarray(L2_conv_w1), np.asarray(L2_conv_w2), np.asarray(L2_conv_w3)], axis=1),
        b3=np.concatenate([np.asarray(L2_conv_b1), np.asarray(L2_conv_b2), np.asarray(L2_conv_b3)]),
        wqv=np.concatenate([qkv[:, 0:HID], qkv[:, 2 * HID:3 * HID]], axis=1),
        wk=qkv[:, HID:2 * HID],
        w_out=np.asarray(L3_conv_w_out),
        b_out=np.asarray(L3_conv_b_out),
        gamma=np.asarray(L3_conv_gamma),
        beta=np.asarray(L3_conv_beta).reshape(KC, P).T,
        ident_in=np.eye(P, dtype=np.float32),
        gmat_in=np.kron(np.eye(P // GN_GROUP, dtype=np.float32),
                        np.full((GN_GROUP, GN_GROUP), 1.0 / GN_GROUP, np.float32)),
    )
    nc = bacc.Bacc("TRN2", target_bir_lowering=False, num_devices=1)
    feeds, args = {}, []
    for name, a in arrays.items():
        a = np.ascontiguousarray(a)
        feeds[name] = a
        args.append(nc.dram_tensor(name, a.shape, mybir.dt.from_np(a.dtype), kind="ExternalInput").ap())
    out = nc.dram_tensor("out", arrays["x"].shape, F32, kind="ExternalOutput").ap()
    build(nc, *args, out)
    return run_bass_kernel_spmd(nc, [feeds], core_ids=[0]).results[0]["out"]
```

```python
from contextlib import ExitStack

import concourse.bass as bass
from concourse import mybir

F32 = mybir.dt.float32
F16 = mybir.dt.float16
BF16 = mybir.dt.bfloat16
U32 = mybir.dt.uint32
ALU = mybir.AluOpType
ACT = mybir.ActivationFunctionType
AX = mybir.AxisListType.X

P = 128
KC = 2
C = KC * P
GT = 4
GW = GT * P
NG = 8
NT = NG * GT
N = NG * GW
CODES = 1024
CK = 32
ROW = 64
HEADS = 4
DH = 32
HID = HEADS * DH
GN_GROUP = C // 32
GN_EPS = 1e-5
LN_EPS = 1e-3
PIECES = 12
BROW = 32
NHALF = 2
UNIT = N // NHALF
ZW = 1024
ZONES = 3
QUADS = 4
TRIO = 3
KAPPA = 256.0


class Step:

    def __init__(self, nc, ctx, name, depth=0):
        self.sem = ctx.enter_context(nc.semaphore(name))
        self.depth = depth

    def after(self, n):
        return n + (self.depth + 1)

    def room(self, n, depth=None):
        return n + 1 + (0 if depth is None else self.depth - depth)


class Group:

    def __init__(self, im, i, c):
        self.slot = c % 2
        self.pair = i + c // 2
        self.n = im * NG + i * 2 + c
        self.occ = im * (NG // 2) + i + c // 2
        self.first = isinstance(i, int) and c == 0
        self.last = isinstance(i, int) and c == NG - 1


def pipeline(eng, im, stages, step, left=0, behind=None, behind_stages=0):

    def static(k):
        return lambda s: Group(im, 0, k - s) if 0 <= k - s < NG else None

    first = 2 if stages <= 3 else 4
    for k in range(first):
        step(static(k))
        if behind is not None:
            behind(static(NG + behind_stages - 1 - first + k))
    with eng.Fori(0, (NG - first) // 2) as i:
        for u in range(2):
            step(lambda s, u=u: Group(im, i, first + u - s))
    for k in range(NG, NG + stages - 1 - left):
        step(static(k))


class Chain:

    def __init__(self, sem, per):
        self.sem, self.per, self.k = sem, per, 0

    def start(self, rnd):
        self.rnd, self.k = rnd, 0

    def link(self, eng, ins):
        self.k += 1
        ins.then_inc(self.sem, 1)
        eng.wait_ge(self.sem, self.rnd * self.per + self.k)

    def end(self):
        assert self.k == self.per, (self.k, self.per)


def build(nc, x, emb, emb_t, wfg, bfg, wh, bh, w3, b3, wqv, wk, w_out, b_out, gamma, beta, ident_in, gmat_in, out):
    B = x.shape[0]
    xv = x.rearrange("b (g u r) w c -> b g (r w) u c", g=NG, u=GT)
    xv_ahead = [xv, xv[1:B]]
    ov = out.rearrange("b (q s u r) w c -> b (r w) q s u c", q=NG // 2, s=2, u=GT)

    with ExitStack() as ctx:
        def sb(name, shape, dt=F32):
            return ctx.enter_context(nc.sbuf_tensor(name, shape, dt))

        def sem(name):
            return ctx.enter_context(nc.semaphore(name))

        def step(name, depth=0):
            s = Step(nc, ctx, name, depth)
            if depth:
                credited.append(s)
            return s

        credited = []
        PS = ctx.enter_context(nc.psum_tensor("PS", [P, 8, 512], F32))

        ident = sb("ident", [P, P])
        gmat = sb("gmat", [P, P])
        ones = sb("ones", [P, P])
        minus_half = sb("minus_half", [P, 96])
        onesel = sb("onesel", [96, 512], BF16)
        mhalf2 = sb("mhalf2", [P, GT])
        e_hi = sb("e_hi", [P, KC, CODES], F16)
        e_lo = sb("e_lo", [P, KC, CODES], F16)
        e_bias = sb("e_bias", [96, CODES], BF16)
        fg_hi = sb("fg_hi", [P, KC, 2 * CK], F16)
        fg_lo = sb("fg_lo", [P, KC, 2 * CK], F16)
        fg_bias = sb("fg_bias", [96, 2 * CK], BF16)
        h_hi = sb("h_hi", [P, KC, C], F16)
        h_lo = sb("h_lo", [P, KC, C], F16)
        h_bias = sb("h_bias", [P, C])
        w3_sb = sb("w3_sb", [P, KC, P])
        b3_sb = sb("b3_sb", [P, 1])
        qv_hi = sb("qv_hi", [P, KC, 2 * HID], F16)
        qv_lo = sb("qv_lo", [P, KC, 2 * HID], F16)
        k_hi = sb("k_hi", [P, KC, HID], F16)
        k_lo = sb("k_lo", [P, KC, HID], F16)
        wo_c = sb("wo_c", [P, C])
        z_bias = sb("z_bias", [96, C], BF16)
        gamma_b = sb("gamma_b", [P, C])
        beta_c = sb("beta_c", [P, KC])

        xin = sb("xin", [P, NG, GT, C])
        XT = sb("XT", [P, KC, NG // 2, 2, GW])
        xn = sb("xn", [P, 2, KC, GW])
        xhi = sb("xhi", [P, 2, KC, GW], F16)
        xlo = sb("xlo", [P, 2, KC, GW], F16)

        stats = sb("stats", [P, KC, NG // 2, 2, 6])
        mv = sb("mv", [P, KC, 2])
        gm = sb("gm", [P, KC])
        dm = sb("dm", [P, KC])
        vv = sb("vv", [P, KC])
        ve = sb("ve", [P, KC])
        gs = sb("gs", [P, KC])
        gt = sb("gt", [P, KC])
        m8 = sb("m8", [P, 2, 8])
        idx = sb("idx", [P, 2 * GT, 8], U32)

        work = sb("work", [P, 6144])
        quant = work[:, 0:2048].rearrange("p (s u c) -> p s u c", s=2, u=GT)
        H = work[:, 0:2048].rearrange("p (s u c) -> p s u c", s=2, u=GT)
        FT = work[0:CK, 2048:3072].rearrange("p (s w n) -> p s w n", s=2, w=2)
        GTm = work[0:CK, 3072:4096].rearrange("p (s w n) -> p s w n", s=2, w=2)
        diag = work[:, 0:1024].rearrange("p (s u n) -> p s u n", s=2, u=GT)
        gated = work[:, 1024:3072].rearrange("p (s k n) -> p s k n", s=2, k=KC)
        qe = work[:, 0:1024].rearrange("p (s u n) -> p s u n", s=2, u=GT)
        qs = work[:, 1024:2048].rearrange("p (s u n) -> p s u n", s=2, u=GT)
        ke = work[:, 2048:3072].rearrange("p (s u n) -> p s u n", s=2, u=GT)
        kt = work[:, 3072:4096].rearrange("p (s u n) -> p s u n", s=2, u=GT)
        xb = work[:, 0:2048].rearrange("p (s k n) -> p s k n", s=2, k=KC)
        Y = work[:, 2048:4096].rearrange("p (s u c) -> p s u c", s=2, u=GT)
        squares = work[:, 4096:6144].rearrange("p (s u c) -> p s u c", s=2, u=GT)
        attn = sb("attn", [P, 2, GT, P])
        yout = sb("yout", [P, 2, GT, C])

        big = sb("big", [P, 12288])
        E = big[:, 0:TRIO * 2048].rearrange("p (s n) -> p s n", s=TRIO)
        lhs_p = big[0:PIECES, 6144:8192].bitcast(BF16)
        rhs_p = big[:, 8192:10240].bitcast(BF16)
        pc = big[:, 10240:10240 + NT * 44].rearrange("p (t k) -> p t k", k=44)
        accs = big[:, 0:1024]
        KTs = big[:, 0:4096].rearrange("p (g s n) -> p g s n", g=NG // 2, s=2)
        V = big[:, 4096:8192].rearrange("p (g s u n) -> p g s u n", g=NG // 2, s=2, u=GT)
        q_hi = big[:, 8192:10240].bitcast(F16).rearrange("p (g s u n) -> p g s u n", g=NG // 2, s=2, u=GT)
        q_lo = big[:, 10240:12288].bitcast(F16).rearrange("p (g s u n) -> p g s u n", g=NG // 2, s=2, u=GT)

        gate = sb("gate", [P, 3, NT])
        gcol = gate[:, 2, :].rearrange("p (q s u) -> p q s u", q=NG // 2, s=2)
        w3s = sb("w3s", [P, KC, 32])
        pb3 = sb("pb3", [P, 1])
        rows3 = big[:, 6144:7168].rearrange("p (b n) -> p b n", b=2)
        s3 = sb("s3", [P, 3, NT])
        x2c = sb("x2c", [P, NT])
        pk = sb("pk", [P, 3, 3, NT], BF16)
        r3 = sb("r3", [P, 2, 3, NT])
        mm2 = sb("mm2", [P, 2])
        mt2 = sb("mt2", [2, 1])
        dg2 = sb("dg2", [2, 2])
        mx2 = sb("mx2", [P, 2])
        ma = sb("ma", [P, 2, NT])
        lhs_s = sb("lhs_s", [P, TRIO, P], BF16)
        w2 = sb("w2", [P, TRIO, 32])
        zero_w = sb("zero_w", [P, P])
        nums = sb("nums", [P, NHALF, QUADS, GT])
        qmx = sb("qmx", [P, 2, GT * HEADS])
        qsum = sb("qsum", [P, 2, 2, GT * HEADS])
        kmx = sb("kmx", [P, NG // 2, 2])
        kneg = sb("kneg", [P, 1])
        ksum = sb("ksum", [P, NG // 2, 2])
        kden = sb("kden", [P, 2])
        ctxd = sb("ctxd", [P, P])
        ctxt = sb("ctxt", [P, P])
        m_hi = sb("m_hi", [P, C], F16)
        m_lo = sb("m_lo", [P, C], F16)
        sq = sb("sq", [P, 2, GT])
        rstd = sb("rstd", [P, 2, 2, GT])

        weights_in = sem("weights_in")
        setup_dve = sem("setup_dve")
        emb_squared = sem("emb_squared")
        setup_pe = sem("setup_pe")
        start = sem("start")
        phase_end = sem("phase_end")
        waits_apart = sem("waits_apart")
        loaded = [sem(f"loaded{g}") for g in range(NG)]
        gathered = [[sem(f"gathered{s}{u}") for u in range(GT)] for s in range(2)]
        stored = [sem(f"stored{s}") for s in range(2)]
        a_turned = step("a_turned", 8)
        a_kept = step("a_kept", 2)
        stats_done = [step(f"stats_done{l}") for l in range(4)]
        mean_ready, mean_ps, var_ready, var_ps, ve_ready, pow_done, gn_ready = (
            step(n) for n in ("mean_ready", "mean_ps", "var_ready", "var_ps", "ve_ready", "pow_done", "gn_ready"))
        first_hi = step("first_hi")
        l0_xn, l0_hi, l0_lo = step("l0_xn"), step("l0_hi"), step("l0_lo", 2)
        l0_scored, l0_maxed, l0_indexed = step("l0_scored", 8), step("l0_maxed"), step("l0_indexed", 2)
        l0_turned, l0_added = step("l0_turned", 2), step("l0_added", 2)
        l1_xn, l1_hi, l1_lo = step("l1_xn"), step("l1_hi"), step("l1_lo", 2)
        l1_fg, l1_fgkept, l1_h, l1_hkept = step("l1_fg"), step("l1_fgkept", 2), step("l1_h", 4), step("l1_hkept", 2)
        l1_scores, l1_tanh, l1_attn = step("l1_scores", 2), step("l1_tanh", 2), step("l1_attn")
        l1_out, l1_added = step("l1_out", 2), step("l1_added", 1)
        w3_scaled, pb3_ps, pb3_ready, l2_proj, l2_rows, rows_turned = (
            step(n) for n in ("w3_scaled", "pb3_ps", "pb3_ready", "l2_proj", "l2_rows", "rows_turned"))
        x0max_in, x0max_t, x0max_d, x0max_b = (step(n) for n in ("x0max_in", "x0max_t", "x0max_d", "x0max_b"))
        pieces_made, pieces_turned, lhs_kept, rhs_kept = (
            step("pieces_made"), step("pieces_turned"), step("lhs_kept", 4), step("rhs_kept", 4))
        exps_in, exps_done, sums_done = step("exps_in"), step("exps_done", ZONES), step("sums_done", 6)
        tile_staged = step("tile_staged")
        acc_kept, acc_turned = step("acc_kept"), step("acc_turned")
        gate_exp, gate_made = step("gate_exp"), step("gate_made")
        g_xn, g_diag, g_diag_last, g_spread = step("g_xn"), step("g_diag"), step("g_diag_last"), step("g_spread", 2)
        g_gated, g_added = step("g_gated", 2), step("g_added", 2)
        l3_xn, l3_hi, l3_lo = step("l3_xn"), step("l3_hi"), step("l3_lo", 2)
        l3_k, l3_kkept, l3_kmax = step("l3_k"), step("l3_kkept", 2), step("l3_kmax", 2)
        l3_qv, l3_vkept = step("l3_qv", 2), step("l3_vkept", 2)
        l3_qmax, l3_qsub, l3_qexp, l3_qsoft = step("l3_qmax"), step("l3_qsub", 2), step("l3_qexp", 2), step("l3_qsoft")
        l3_qt, l3_qhi, l3_qlo = step("l3_qt", 2), step("l3_qhi", 2), step("l3_qlo", 2)
        kneg_ready, l3_kexp, l3_kturned, l3_kback = step("kneg_ready"), step("l3_kexp"), step("l3_kturned", 2), step("l3_kback", 2)
        l3_ctx, ctx_done, ctxd_ready, ctxt_ps, ctxt_ready, m_ps, mhi_ready, mlo_ready = (
            step("l3_ctx", 2), *(step(n) for n in ("ctx_done", "ctxd_ready", "ctxt_ps", "ctxt_ready", "m_ps", "mhi_ready", "mlo_ready")))
        f_xb, f_turned, f_z, f_sq = step("f_xb"), step("f_turned", 2), step("f_z"), step("f_sq", 2)
        f_ve, f_rstd, f_y, f_out = step("f_ve"), step("f_rstd"), step("f_y", 2), step("f_out", 2)
        gn_chain = Chain(sem("gn_chain"), 4)
        small_chain = Chain(sem("small_chain"), 10)
        gate_chain = Chain(sem("gate_chain"), 4)
        q_chain = Chain(sem("q_chain"), 2)
        k_chain = Chain(sem("k_chain"), 3)

        PHASES = 8
        block = ctx.enter_context(nc.Block())

        def qv_ps(g):
            return PS[:, 2 + 2 * g.slot:4 + 2 * g.slot, :].rearrange("p a (u n) -> p (a u) n", u=2)

        def z_ps(g):
            return PS[:, 2 * g.slot:2 * g.slot + 2, :].rearrange("p a (u n) -> p (a u) n", u=2)

        def xt_ps(g):
            return PS[:, 4 + 2 * g.slot:6 + 2 * g.slot, :].rearrange("p a (u n) -> p (a u) n", u=2)

        def apart(eng):
            eng.sem_inc(waits_apart, 1)

        def barrier(eng, im, phase):
            apart(eng)
            eng.drain().then_inc(phase_end, 1)
            eng.wait_ge(phase_end, im * (4 * PHASES) + 4 * (phase + 1))
            apart(eng)

        wst = xin[:, :, :, :].rearrange("p g u c -> p (g u c)")
        emb_f = wst[:, 0:2048].rearrange("p (k n) -> p k n", k=KC)
        emb_q = wst[:, 2048:4096].rearrange("p (k n) -> p k n", k=KC)
        wfg_f = XT[:, 0, 0, 0, 0:128].rearrange("p (k n) -> p k n", k=KC)
        xt_w = XT[:, :, :, :, :].rearrange("p k g s n -> p (k g s n)")
        wfg_f = xt_w[:, 0:128].rearrange("p (k n) -> p k n", k=KC)
        wh_f = xt_w[:, 128:640].rearrange("p (k n) -> p k n", k=KC)
        wqv_f = xt_w[:, 640:1152].rearrange("p (k n) -> p k n", k=KC)
        wk_f = xt_w[:, 1152:1408].rearrange("p (k n) -> p k n", k=KC)
        rows_f = xt_w[0:96, 1408:1408 + CODES]
        rows_r = xt_w[0:96, 2432:2432 + CODES]
        bfg_f = xt_w[0:96, 3456:3520]
        bo_f = xt_w[0:96, 3520:3776]
        wmean = xt_w[:, 3776:3778]
        wo_f = xt_w[:, 3800:4056]
        NW = 15

        @block.sync
        def _(sp):
            for dst, src in (
                (emb_f, emb.rearrange("(k p) n -> p k n", p=P)),
                (wfg_f, wfg.rearrange("(k p) n -> p k n", p=P)),
                (wh_f, wh.rearrange("(k p) n -> p k n", p=P)),
                (wqv_f, wqv.rearrange("(k p) n -> p k n", p=P)),
                (wk_f, wk.rearrange("(k p) n -> p k n", p=P)),
                (w3_sb[:, :, :], w3.rearrange("(k p) n -> p k n", p=P)),
                (wo_f, w_out),
                (h_bias[:, :], bh.partition_broadcast(P)),
                (b3_sb[:, :], b3),
                (gamma_b[:, :], gamma.partition_broadcast(P)),
                (beta_c[:, :], beta),
                (bfg_f, bfg.partition_broadcast(96)),
                (bo_f, b_out.partition_broadcast(96)),
                (ident[:, :], ident_in),
                (gmat[:, :], gmat_in),
            ):
                sp.dma_start(dst, src).then_inc(weights_in, 16)
            for s in credited:
                sp.sem_inc(s.sem, s.depth)
            for s in range(2):
                sp.sem_inc(stored[s], 16)
            sp.sem_inc(start, 1)
            sp.wait_ge(start, 4)

            def load(im, ahead):
                for g in range(NG):
                    sp.wait_ge(a_turned.sem, a_turned.room(im * NG + ahead * NG + g))
                    apart(sp)
                    sp.dma_start(xin[:, g, :, :], xv_ahead[ahead][im, g]).then_inc(loaded[g], 16)

            def store(im):
                def one(at):
                    g = at(0)
                    sp.wait_ge(f_out.sem, f_out.after(g.n))
                    apart(sp)
                    sp.dma_start(ov[im, :, g.pair, g.slot, :, :], yout[:, g.slot, :, :]).then_inc(stored[g.slot], 16)

                pipeline(sp, im, 1, one)

            load(0, 0)
            if B > 1:
                with sp.Fori(0, B - 1) as im:
                    load(im, 1)
                    store(im)
            store(B - 1)
            for s in range(2):
                sp.wait_ge(stored[s], 16 + 16 * B * NG // 2)

        @block.gpsimd
        def _(pool):
            pool.sem_inc(start, 1)
            pool.wait_ge(start, 4)
            with pool.Fori(0, B) as im:
                def gn(layer):
                    r = im * 4 + layer
                    pool.wait_ge(ve_ready.sem, ve_ready.after(r))
                    nc.gpsimd.tensor_tensor(gs[:, :], ve[:, :], mhalf2[:, 0:KC], ALU.pow).then_inc(pow_done.sem, 1)

                def low(g, hi, lo, free):
                    if g.first:
                        pool.wait_ge(lo.sem, lo.after(g.n))
                        return
                    pool.wait_ge(hi.sem, hi.after(g.n))
                    pool.wait_ge(*free)
                    nc.gpsimd.tensor_tensor(xlo[:, g.slot, :, :], xn[:, g.slot, :, :], xhi[:, g.slot, :, :],
                                    ALU.subtract).then_inc(lo.sem, 1)

                barrier(pool, im, 0)
                gn(0)

                def l0(at):
                    g = at(0)
                    if g is not None:
                        low(g, l0_hi, l0_lo, (l0_scored.sem, l0_scored.room(g.n * GT + GT - 1)))
                    g = at(1)
                    if g is None:
                        return
                    for u in range(GT):
                        if u == 0:
                            pool.wait_ge(l0_turned.sem, l0_turned.room(g.n))
                        pool.wait_ge(l0_indexed.sem, l0_indexed.after(g.n * GT + u))
                        apart(pool)
                        nc.gpsimd.indirect_dma_start(
                            quant[:, g.slot, u, :], None, emb_t,
                            bass.IndirectOffsetOnAxis(ap=idx[:, g.slot * GT + u, 0:1], axis=0),
                        ).then_inc(gathered[g.slot][u], 16)

                pipeline(pool, im, 2, l0)
                barrier(pool, im, 1)
                gn(1)

                def l1(at):
                    g = at(0)
                    low(g, l1_hi, l1_lo, (l1_h.sem, l1_h.room(g.n * 2 + 1)))

                pipeline(pool, im, 1, l1)
                barrier(pool, im, 2)
                gn(2)
                barrier(pool, im, 3)
                barrier(pool, im, 4)

                def l2_add(at):
                    g = at(0)
                    if g is None:
                        return
                    pool.wait_ge(g_gated.sem, g_gated.after(g.n))
                    nc.gpsimd.tensor_tensor(XT[:, :, g.pair, g.slot, :], XT[:, :, g.pair, g.slot, :],
                                            gated[:, g.slot, :, :], ALU.add).then_inc(g_added.sem, 1)

                pipeline(pool, im, 1, l2_add)
                barrier(pool, im, 5)
                gn(3)

                def l3(at):
                    g = at(0)
                    low(g, l3_hi, l3_lo, (l3_qv.sem, l3_qv.room(g.n)))

                pipeline(pool, im, 1, l3)
                barrier(pool, im, 6)

                def l3_pow(at):
                    g = at(1)
                    if g is not None:
                        pool.wait_ge(f_ve.sem, f_ve.after(g.n))
                        nc.gpsimd.tensor_tensor(rstd[:, g.slot, 1, :], rstd[:, g.slot, 0, :], mhalf2[:, :],
                                                ALU.pow).then_inc(f_rstd.sem, 1)
                    g = at(0)
                    if g is not None:
                        pool.wait_ge(f_turned.sem, f_turned.room(g.n))
                        nc.gpsimd.tensor_tensor(xb[:, g.slot, :, :], XT[:, :, g.pair, g.slot, :],
                                                beta_c[:, :].unsqueeze(2).broadcast_to([P, KC, GW]),
                                                ALU.add).then_inc(f_xb.sem, 1)

                pipeline(pool, im, 2, l3_pow)
                barrier(pool, im, 7)

        @block.scalar
        def _(act):
            act.sem_inc(start, 1)
            act.wait_ge(start, 4)
            with act.Fori(0, B) as im:
                def normed(g, made, free):
                    act.wait_ge(*free)
                    for k in range(KC):
                        last = nc.scalar.activation(xn[:, g.slot, k, :], XT[:, k, g.pair, g.slot, :], ACT.Identity,
                                                    scale=gs[:, k:k + 1], bias=gt[:, k:k + 1])
                    last.then_inc(made.sem, 1)

                def head(g, made, hi, free):
                    if g.first:
                        return
                    act.wait_ge(*free)
                    act.wait_ge(made.sem, made.after(g.n))
                    nc.scalar.activation(xhi[:, g.slot, :, :], xn[:, g.slot, :, :], ACT.Identity).then_inc(hi.sem, 1)

                def norm(g, made, free, hi, hi_free):
                    normed(g, made, free)
                    head(g, made, hi, hi_free)

                for s in range(NG):
                    n = im * NG + s
                    b = 2 * (s % 2)
                    act.wait_ge(a_turned.sem, a_turned.after(n))
                    nc.scalar.activation(XT[:, :, s // 2, s % 2, :], PS[:, b:b + 2, :], ACT.Identity).then_inc(a_kept.sem, 1)
                barrier(act, im, 0)

                def l0(at):
                    g = at(0)
                    if g is not None:
                        norm(g, l0_xn, (l0_lo.sem, l0_lo.room(g.n)), l0_hi,
                             (l0_scored.sem, l0_scored.room(g.n * GT + GT - 1)))

                act.wait_ge(gn_ready.sem, gn_ready.after(im * 4))
                pipeline(act, im, 1, l0)
                barrier(act, im, 1)

                def l1(at):
                    g = at(0)
                    if g is not None:
                        norm(g, l1_xn, (l1_lo.sem, l1_lo.room(g.n)), l1_hi, (l1_h.sem, l1_h.room(g.n * 2 + 1)))
                    g = at(1)
                    if g is not None:
                        act.wait_ge(l1_fg.sem, l1_fg.after(g.n))
                        act.wait_ge(l1_scores.sem, l1_scores.room(g.n))
                        for w in range(2):
                            r = 2 * CK * w
                            nc.scalar.activation(FT[:, g.slot, w, :], PS[r:r + CK, g.slot, 0:2 * P], ACT.Identity)
                            last = nc.scalar.activation(GTm[:, g.slot, w, :], PS[r + CK:r + 2 * CK, g.slot, 0:2 * P],
                                                        ACT.Identity)
                        last.then_inc(l1_fgkept.sem, 1)
                        act.wait_ge(l1_scores.sem, l1_scores.after(g.n))
                        act.wait_ge(l1_out.sem, l1_out.room(g.n))
                        src = PS[:, 2 + g.slot, :].rearrange("p (u n) -> p u n", u=GT)
                        for r in range(P // ROW):
                            rr = slice(r * ROW, (r + 1) * ROW)
                            last = nc.scalar.activation(attn[rr, g.slot, :, rr], src[rr, :, rr], ACT.Tanh, scale=0.5)
                        last.then_inc(l1_tanh.sem, 1)

                act.wait_ge(gn_ready.sem, gn_ready.after(im * 4 + 1))
                pipeline(act, im, 2, l1)
                barrier(act, im, 2)

                for b in range(2):
                    act.wait_ge(l2_proj.sem, l2_proj.after(im * 2 + b))
                    nc.scalar.activation(rows3[:, b, :], PS[:, b, :], ACT.Identity, bias=pb3[:, :]).then_inc(l2_rows.sem, 1)
                for s in range(NG):
                    n = im * NG + s
                    act.wait_ge(pieces_turned.sem, pieces_turned.after(n))
                    nc.scalar.activation(lhs_p[:, s * GW:(s + 1) * GW], PS[0:PIECES, s % 4, :],
                                         ACT.Identity).then_inc(lhs_kept.sem, 1)
                barrier(act, im, 3)

                def exps(i, j, tt):
                    for z in range(4):
                        c = (im * NT + i * TRIO + tt) * 4 + z
                        zone = (tt * 4 + z) % ZONES
                        e = (tt * 2 + z // 2) % TRIO
                        act.wait_ge(exps_in.sem, exps_in.after(c))
                        if z % 2 == 0:
                            act.wait_ge(sums_done.sem, sums_done.room((im * NT + i * TRIO + tt) * 2 + z // 2, TRIO))
                        nc.scalar.activation(E[:, e, (z % 2) * ZW:(z % 2 + 1) * ZW],
                                             PS[:, 2 * zone:2 * zone + 2, :].rearrange("p a n -> p (a n)"),
                                             ACT.Exp).then_inc(exps_done.sem, 1)

                with act.Fori(0, NT // TRIO) as i:
                    for tt in range(TRIO):
                        exps(i, tt, tt)
                for tt in range(NT - NT // TRIO * TRIO):
                    exps(NT // TRIO, tt, tt)
                act.wait_ge(sums_done.sem, sums_done.after((im + 1) * (NT * NHALF) - 1))
                nc.scalar.activation(accs, PS[:, 6:8, :].rearrange("p a n -> p (a n)"), ACT.Identity).then_inc(acc_kept.sem, 1)
                act.wait_ge(gate_made.sem, gate_made.after(im))
                nc.scalar.activation(gate[:, 1, :], gate[:, 0, :], ACT.Exp, scale=-1.0).then_inc(gate_exp.sem, 1)
                barrier(act, im, 4)

                def l2_gate(at):
                    g = at(0)
                    if g is not None:
                        act.wait_ge(g_spread.sem, g_spread.room(g.n))
                        for u in range(GT - 1):
                            last = nc.scalar.activation(diag[:, g.slot, u, :], ident[:, :], ACT.Identity,
                                                        scale=gcol[:, g.pair, g.slot, u:u + 1])
                        last.then_inc(g_diag.sem, 1)
                        normed(g, g_xn, (g_gated.sem, g_gated.room(g.n)))

                pipeline(act, im, 1, l2_gate)
                barrier(act, im, 5)

                def l3(at):
                    g = at(0)
                    if g is not None:
                        normed(g, l3_xn, (l3_lo.sem, l3_lo.room(g.n)))
                    g = at(2)
                    if g is not None:
                        act.wait_ge(l3_qv.sem, l3_qv.after(g.n))
                        nc.scalar.activation(KTs[:, g.pair, g.slot, :], PS[:, g.slot, :], ACT.Identity).then_inc(l3_kkept.sem, 1)
                        nc.scalar.activation(V[:, g.pair, g.slot, :, :], qv_ps(g)[:, :, HID:2 * HID],
                                             ACT.Identity).then_inc(l3_vkept.sem, 1)
                    g = at(0)
                    if g is not None:
                        head(g, l3_xn, l3_hi, (l3_qv.sem, l3_qv.room(g.n)))
                    g = at(3)
                    if g is not None:
                        act.wait_ge(l3_qsub.sem, l3_qsub.after(g.n))
                        nc.scalar.activation(qe[:, g.slot, :, :], qe[:, g.slot, :, :], ACT.Exp).then_inc(l3_qexp.sem, 1)
                    g = at(4)
                    if g is not None:
                        act.wait_ge(l3_qt.sem, l3_qt.after(g.n))
                        nc.scalar.activation(q_hi[:, g.pair, g.slot, :, :],
                                             PS[:, 6 + g.slot, :].rearrange("p (u n) -> p u n", u=GT),
                                             ACT.Identity).then_inc(l3_qhi.sem, 1)

                act.wait_ge(gn_ready.sem, gn_ready.after(im * 4 + 3))
                pipeline(act, im, 5, l3, left=2)

                def l3_keys(at):
                    g = at(0)
                    if g is not None:
                        act.wait_ge(kneg_ready.sem, kneg_ready.after(im))
                        act.wait_ge(l3_kturned.sem, l3_kturned.room(g.n))
                        nc.scalar.activation(ke[:, g.slot, :, :].rearrange("p u n -> p (u n)"),
                                             KTs[:, g.pair, g.slot, :], ACT.Exp, bias=kneg[:, :],
                                             accum_out=ksum[:, g.pair, g.slot:g.slot + 1]).then_inc(l3_kexp.sem, 1)

                pipeline(act, im, 1, l3_keys, behind=l3, behind_stages=5)
                act.wait_ge(m_ps.sem, m_ps.after(im))
                act.wait_ge(ctxd_ready.sem, ctxd_ready.after(im))
                nc.scalar.activation(m_hi[:, :], PS[:, 5, 0:C], ACT.Identity).then_inc(mhi_ready.sem, 1)
                barrier(act, im, 6)

                def final(at):
                    g = at(1)
                    if g is not None:
                        act.wait_ge(f_z.sem, f_z.after(g.n))
                        act.wait_ge(f_y.sem, f_y.room(g.n))
                        for u in range(GT):
                            last = nc.scalar.activation(squares[:, g.slot, u, :], z_ps(g)[:, u, :], ACT.Square,
                                                        accum_out=sq[:, g.slot, u:u + 1])
                        last.then_inc(f_sq.sem, 1)

                pipeline(act, im, 2, final)
                barrier(act, im, 7)

        @block.vector
        def _(dve):
            v = nc.vector
            chain = [0]

            def link(ins):
                chain[0] += 1
                ins.then_inc(setup_dve, 1)
                dve.wait_ge(setup_dve, chain[0])

            def pieces(dst, src, rem, w):
                for j in range(3):
                    rr = slice(32 * j, 32 * j + 32)
                    link(v.tensor_copy(dst[rr, 0:w], src[rr, 0:w]))
                    if j < 2:
                        for q in range(j + 1, 3):
                            tail = slice(32 * q, 32 * q + 32)
                            link(v.tensor_copy(rem[tail, 0:w], dst[rr, 0:w]))
                            link(v.tensor_tensor(src[tail, 0:w], src[tail, 0:w], rem[tail, 0:w], ALU.subtract))

            for t, val in ((ones, 1.0), (minus_half, -0.5), (mhalf2, -0.5), (attn, 0.0), (w2, 0.0), (zero_w, 0.0), (lhs_s, 0.0),
                           (ctxd, 0.0), (onesel, 0.0)):
                link(v.memset(t[:], val))
            for j in range(3):
                link(v.memset(onesel[32 * j:32 * j + 1, :], 1.0))
            link(v.memset(w2[:, :, 1:2], 1.0))
            dve.wait_ge(weights_in, 16 * NW)
            for src, hi, lo in ((emb_f, e_hi, e_lo), (wfg_f, fg_hi, fg_lo), (wh_f, h_hi, h_lo), (wqv_f, qv_hi, qv_lo),
                                (wk_f, k_hi, k_lo)):
                link(v.tensor_copy(hi[:], src))
                link(v.tensor_tensor(lo[:], src, hi[:], ALU.subtract))
            v.tensor_tensor(emb_q, emb_f, emb_f, ALU.mult).then_inc(emb_squared, 1)
            dve.wait_ge(setup_pe, 1)
            link(v.tensor_copy(rows_f, PS[0:96, 0:2, :].rearrange("p a n -> p (a n)")))
            pieces(e_bias, rows_f, rows_r, CODES)
            pieces(fg_bias, bfg_f, rows_r, 2 * CK)
            link(v.tensor_reduce(wmean[:, 0:1], wo_f, AX, ALU.add))
            link(v.tensor_scalar(wmean[:, 1:2], wmean[:, 0:1], 1.0 / C, None, ALU.mult))
            link(v.tensor_scalar(wo_c[:, :], wo_f, wmean[:, 1:2], None, ALU.subtract))
            link(v.tensor_reduce(wmean[0:96, 0:1], bo_f, AX, ALU.add))
            link(v.tensor_scalar(wmean[0:96, 1:2], wmean[0:96, 0:1], 1.0 / C, None, ALU.mult))
            link(v.tensor_scalar(bo_f, bo_f, wmean[0:96, 1:2], KAPPA, ALU.subtract, ALU.mult))
            pieces(z_bias, bo_f, rows_r, C)
            dve.sem_inc(start, 1)
            dve.wait_ge(start, 4)

            with dve.Fori(0, B) as im:
                def gn(layer, stat):
                    r = im * 4 + layer
                    gn_chain.start(r)
                    dve.wait_ge(stat.sem, stat.after(im * NG + NG - 1))
                    for k in range(KC):
                        apart(dve)
                        gn_chain.link(dve, v.bn_aggr(mv[:, k, :], stats[:, k, :, :, :].rearrange("p g s n -> p (g s n)")))
                    v.tensor_copy(dm[:, :], mv[:, :, 0]).then_inc(mean_ready.sem, 1)
                    dve.wait_ge(mean_ps.sem, mean_ps.after(r))
                    dve.wait_ge(mean_ready.sem, mean_ready.after(r))
                    v.tensor_copy(gm[:, :], PS[:, 7, 0:KC])
                    gn_chain.link(dve, v.tensor_tensor(dm[:, :], dm[:, :], PS[:, 7, 0:KC], ALU.subtract))
                    gn_chain.link(dve, v.tensor_tensor(vv[:, :], dm[:, :], dm[:, :], ALU.mult))
                    v.tensor_tensor(vv[:, :], vv[:, :], mv[:, :, 1], ALU.add).then_inc(var_ready.sem, 1)
                    dve.wait_ge(var_ps.sem, var_ps.after(r))
                    v.tensor_scalar(ve[:, :], PS[:, 7, 4:4 + KC], GN_EPS, None, ALU.add).then_inc(ve_ready.sem, 1)
                    dve.wait_ge(pow_done.sem, pow_done.after(r))
                    v.scalar_tensor_tensor(out=gt[:, :], in0=gm[:, :], scalar=-1.0, in1=gs[:, :], op0=ALU.mult,
                                           op1=ALU.mult).then_inc(gn_ready.sem, 1)
                    gn_chain.end()

                def first_group(layer, made, hi, lo):
                    g = Group(im, 0, 0)
                    dve.wait_ge(gn_ready.sem, gn_ready.after(im * 4 + layer))
                    for k in range(KC):
                        last = v.tensor_scalar(xhi[:, 0, k, :], XT[:, k, 0, 0, :], gs[:, k:k + 1], gt[:, k:k + 1],
                                               ALU.mult, ALU.add)
                        last.then_inc((hi, first_hi)[k].sem, 1)
                    dve.wait_ge(made.sem, made.after(g.n))
                    dve.wait_ge(first_hi.sem, first_hi.after(im * 3 + (0, 1, None, 2)[layer]))
                    v.tensor_tensor(xlo[:, 0, :, :], xn[:, 0, :, :], xhi[:, 0, :, :], ALU.subtract).then_inc(lo.sem, 1)

                def stat(g, done):
                    for k in range(KC):
                        last = v.bn_stats(stats[:, k, g.pair, g.slot, :], XT[:, k, g.pair, g.slot, :])
                    last.then_inc(done.sem, 1)

                for s in range(NG):
                    g = Group(im, 0, s)
                    dve.wait_ge(a_kept.sem, a_kept.after(g.n))
                    stat(g, stats_done[0])
                barrier(dve, im, 0)
                gn(0, stats_done[0])
                first_group(0, l0_xn, l0_hi, l0_lo)

                def l0(at):
                    g, add = at(1), at(3)
                    if add is not None:
                        dve.wait_ge(l0_turned.sem, l0_turned.after(add.n))

                    def quarter(u):
                        k = u % 2
                        here = XT[:, k, add.pair, add.slot, :]
                        if u < 2:
                            last = v.tensor_tensor(here, here, PS[:, 4 + 2 * add.slot + k, :], ALU.add)
                        else:
                            last = v.bn_stats(stats[:, k, add.pair, add.slot, :], here)
                        if k == 1:
                            last.then_inc((l0_added if u == 1 else stats_done[1]).sem, 1)

                    for u in range(GT):
                        if g is not None:
                            t = g.n * GT + u
                            b = 2 * (u % 2)
                            scores = PS[:, b:b + 2, :].rearrange("p a n -> p (a n)")
                            dve.wait_ge(l0_scored.sem, l0_scored.after(t))
                            apart(dve)
                            v.max(m8[:, u % 2, :], scores).then_inc(l0_maxed.sem, 1)
                        if add is not None:
                            if u == 2:
                                dve.wait_ge(l0_added.sem, l0_added.after(add.n))
                            quarter(u)
                        if g is not None:
                            dve.wait_ge(l0_maxed.sem, l0_maxed.after(t))
                            apart(dve)
                            v.max_index(idx[:, g.slot * GT + u, :], m8[:, u % 2, :], scores).then_inc(l0_indexed.sem, 1)

                pipeline(dve, im, 4, l0)
                barrier(dve, im, 1)
                gn(1, stats_done[1])
                first_group(1, l1_xn, l1_hi, l1_lo)

                def l1(at):
                    g = at(1)
                    if g is not None:
                        dve.wait_ge(l1_out.sem, l1_out.room(g.n))
                        for w in range(2):
                            dve.wait_ge(l1_h.sem, l1_h.after(g.n * 2 + w))
                            v.tensor_tensor(H[:, g.slot, 2 * w:2 * w + 2, :],
                                            PS[:, 4 + w, :].rearrange("p (u n) -> p u n", u=2),
                                            h_bias[:, :].unsqueeze(1).broadcast_to([P, 2, C]),
                                            ALU.add).then_inc(l1_hkept.sem, 1)
                        dve.wait_ge(l1_tanh.sem, l1_tanh.after(g.n))
                        for r in range(P // ROW):
                            rr = slice(r * ROW, (r + 1) * ROW)
                            last = v.tensor_scalar(attn[rr, g.slot, :, rr], attn[rr, g.slot, :, rr], 0.5, 0.5,
                                                   ALU.mult, ALU.add)
                        last.then_inc(l1_attn.sem, 1)
                    g = at(2)
                    if g is not None:
                        dve.wait_ge(l1_out.sem, l1_out.after(g.n))
                        here = XT[:, :, g.pair, g.slot, :]
                        v.tensor_tensor(here, here, PS[:, 6:8, :], ALU.add).then_inc(l1_added.sem, 1)
                        dve.wait_ge(l1_added.sem, l1_added.after(g.n))
                        stat(g, stats_done[2])

                pipeline(dve, im, 3, l1)
                barrier(dve, im, 2)
                gn(2, stats_done[2])

                for k in range(KC):
                    last = v.tensor_scalar(w3s[:, k, :], w3_sb[:, k, 0:32], gs[:, k:k + 1], None, ALU.mult)
                last.then_inc(w3_scaled.sem, 1)
                v.memset(big[:, 8192:10240], 0.0)
                dve.wait_ge(pb3_ps.sem, pb3_ps.after(im))
                v.tensor_tensor(pb3[:, :], PS[:, 2, 0:1], b3_sb[:, :], ALU.add).then_inc(pb3_ready.sem, 1)
                small_chain.start(im)
                sc = small_chain
                dve.wait_ge(rows_turned.sem, rows_turned.after(im))
                turned = PS[:, 4:6, :].rearrange("p b (j q r) -> p b q j r", j=GT, q=QUADS)

                def column(to, r):
                    to = to.rearrange("p (b q j) -> p b q j", b=2, q=QUADS)
                    for b in range(2):
                        last = v.tensor_copy(to[:, b, :, :], turned[:, b, :, :, r])
                    return last

                column(x2c[:, :], 2)
                column(s3[:, 0, :], 0)
                sc.link(dve, column(s3[:, 1, :], 1))
                v.tensor_reduce(mm2[:, 0:1], s3[:, 0, :], AX, ALU.max)
                v.tensor_reduce(mm2[:, 1:2], s3[:, 0, :], AX, ALU.min, negate=True).then_inc(x0max_in.sem, 1)
                dve.wait_ge(x0max_t.sem, x0max_t.after(im))
                sc.link(dve, v.tensor_reduce(mt2[:, :], PS[0:2, 0, 0:P], AX, ALU.max))
                v.tensor_scalar(dg2[:, :], ident[0:2, 0:2], mt2[:, 0:1], None, ALU.mult).then_inc(x0max_d.sem, 1)
                dve.wait_ge(x0max_b.sem, x0max_b.after(im))
                sc.link(dve, v.tensor_copy(mx2[:, :], PS[:, 1, 0:2]))
                v.tensor_scalar(ma[:, 0, :], s3[:, 1, :], mx2[:, 0:1], None, ALU.mult)
                sc.link(dve, v.tensor_scalar(ma[:, 1, :], s3[:, 1, :], mx2[:, 1:2], -1.0, ALU.mult, ALU.mult))
                sc.link(dve, v.tensor_tensor(s3[:, 2, :], ma[:, 0, :], ma[:, 1, :], ALU.max))
                sc.link(dve, v.tensor_copy(pk[:, 0, :, :], s3[:, :, :]))
                sc.link(dve, v.tensor_tensor(r3[:, 0, :, :], s3[:, :, :], pk[:, 0, :, :], ALU.subtract))
                sc.link(dve, v.tensor_copy(pk[:, 1, :, :], r3[:, 0, :, :]))
                sc.link(dve, v.tensor_tensor(r3[:, 1, :, :], r3[:, 0, :, :], pk[:, 1, :, :], ALU.subtract))
                sc.link(dve, v.tensor_copy(pk[:, 2, :, :], r3[:, 1, :, :]))
                v.memset(pc[:, :, PIECES:BROW], 0.0)
                v.memset(pc[:, :, 9:PIECES], -1.0)
                for j in range(3):
                    v.tensor_copy(pc[:, :, 3 * j:3 * j + 3],
                                  pk[:, j, 0, :].unsqueeze(2).broadcast_to([P, NT, 3]))
                    v.tensor_copy(pc[:, :, BROW + j:BROW + 9:3],
                                  pk[:, j, 1, :].unsqueeze(2).broadcast_to([P, NT, 3]))
                    last = v.tensor_copy(pc[:, :, BROW + 9 + j], pk[:, j, 2, :])
                last.then_inc(pieces_made.sem, 1)
                sc.end()
                for s in range(NG):
                    n = im * NG + s
                    dve.wait_ge(pieces_turned.sem, pieces_turned.after(n))
                    v.tensor_copy(rhs_p[0:PIECES, s * GW:(s + 1) * GW],
                                  PS[BROW:BROW + PIECES, s % 4, :]).then_inc(rhs_kept.sem, 1)
                barrier(dve, im, 3)

                body = NT // TRIO
                lhs_tiles = lhs_p[:, 0:body * TRIO * P].rearrange("p (i t n) -> p i t n", t=TRIO, n=P)
                x2_trio = x2c[:, 0:body * TRIO].rearrange("p (i t) -> p i t", t=TRIO)
                with dve.Fori(0, body) as i:
                    for tt in range(TRIO):
                        dve.wait_ge(sums_done.sem, sums_done.room((im * NT + i * TRIO + tt) * 2 + 1))
                        v.tensor_copy(lhs_s[0:PIECES, tt, :], lhs_tiles[:, i, tt, :])
                        v.tensor_copy(w2[:, tt, 0:1], x2_trio[:, i, tt:tt + 1]).then_inc(tile_staged.sem, 1)
                for tt in range(NT - body * TRIO):
                    dve.wait_ge(sums_done.sem, sums_done.room((im * NT + body * TRIO + tt) * 2 + 1))
                    t = body * TRIO + tt
                    v.tensor_copy(lhs_s[0:PIECES, tt, :], lhs_p[:, t * P:(t + 1) * P])
                    v.tensor_copy(w2[:, tt, 0:1], x2c[:, t:t + 1]).then_inc(tile_staged.sem, 1)

                gate_chain.start(im)
                gc = gate_chain
                dve.wait_ge(acc_turned.sem, acc_turned.after(im))
                at_ps = PS[:, 0:NHALF, :].rearrange("p f (j q r) -> p f q j r", j=GT, q=QUADS)
                gview = gate[:, :, :].rearrange("p a (f q j) -> p a f q j", f=NHALF, q=QUADS)
                for f in range(NHALF):
                    last = v.tensor_copy(nums[:, f, :, :], at_ps[:, f, :, :, 1])
                gc.link(dve, last)
                gc.link(dve, v.reciprocal(nums[:, :, :, :], nums[:, :, :, :]))
                for f in range(NHALF):
                    last = v.tensor_tensor(gview[:, 0, f, :, :], at_ps[:, f, :, :, 0], nums[:, f, :, :], ALU.mult)
                last.then_inc(gate_made.sem, 1)
                dve.wait_ge(gate_exp.sem, gate_exp.after(im))
                gc.link(dve, v.tensor_scalar(gate[:, 1, :], gate[:, 1, :], 1.0, None, ALU.add))
                gc.link(dve, v.reciprocal(gate[:, 2, :], gate[:, 1, :]))
                gc.end()
                barrier(dve, im, 4)

                def l2_gate(at):
                    g = at(0)
                    if g is not None:
                        dve.wait_ge(g_spread.sem, g_spread.room(g.n))
                        v.tensor_scalar(diag[:, g.slot, GT - 1, :], ident[:, :], gcol[:, g.pair, g.slot, GT - 1:GT], None,
                                        ALU.mult).then_inc(g_diag_last.sem, 1)
                    g = at(1)
                    if g is not None:
                        dve.wait_ge(g_xn.sem, g_xn.after(g.n))
                        dve.wait_ge(g_spread.sem, g_spread.after(g.n))
                        dve.wait_ge(g_added.sem, g_added.room(g.n))
                        v.tensor_tensor(gated[:, g.slot, :, :], xn[:, g.slot, :, :],
                                        PS[:, g.slot, :].unsqueeze(1).broadcast_to([P, KC, GW]),
                                        ALU.mult).then_inc(g_gated.sem, 1)
                    g = at(2)
                    if g is not None:
                        dve.wait_ge(g_added.sem, g_added.after(g.n))
                        stat(g, stats_done[3])

                pipeline(dve, im, 3, l2_gate)
                barrier(dve, im, 5)
                gn(3, stats_done[3])
                first_group(3, l3_xn, l3_hi, l3_lo)

                def l3(at):
                    g = at(2)
                    if g is not None:
                        dve.wait_ge(l3_vkept.sem, l3_vkept.after(g.n))
                        q_ps = qv_ps(g)[:, :, 0:HID].rearrange("p u (h d) -> p u h d", h=HEADS)
                        qm = qmx[:, g.slot, :].rearrange("p (u h) -> p u h", u=GT)
                        v.tensor_reduce(qm, q_ps, AX, ALU.max).then_inc(l3_qmax.sem, 1)
                        dve.wait_ge(l3_qmax.sem, l3_qmax.after(g.n))
                        v.tensor_tensor(qe[:, g.slot, :, :].rearrange("p u (h d) -> p u h d", h=HEADS), q_ps,
                                        qm.unsqueeze(3).broadcast_to([P, GT, HEADS, DH]),
                                        ALU.subtract).then_inc(l3_qsub.sem, 1)
                    g = at(2)
                    if g is not None:
                        dve.wait_ge(l3_kkept.sem, l3_kkept.after(g.n))
                        v.tensor_reduce(kmx[:, g.pair, g.slot:g.slot + 1], KTs[:, g.pair, g.slot, :], AX,
                                        ALU.max).then_inc(l3_kmax.sem, 1)
                        if g.last:
                            dve.wait_ge(l3_kmax.sem, l3_kmax.after(g.n))
                            v.tensor_reduce(kneg[:, :], kmx[:, :, :].rearrange("p g s -> p (g s)"), AX, ALU.max,
                                            negate=True).then_inc(kneg_ready.sem, 1)
                    g = at(4)
                    if g is not None:
                        dve.wait_ge(l3_qhi.sem, l3_qhi.after(g.n))
                        v.tensor_tensor(q_lo[:, g.pair, g.slot, :, :],
                                        PS[:, 6 + g.slot, :].rearrange("p (u n) -> p u n", u=GT),
                                        q_hi[:, g.pair, g.slot, :, :], ALU.subtract).then_inc(l3_qlo.sem, 1)
                    g = at(3)
                    if g is not None:
                        dve.wait_ge(l3_qexp.sem, l3_qexp.after(g.n))
                        q_chain.start(g.n)
                        flat = qe[:, g.slot, :, :].rearrange("p u (h d) -> p (u h) d", h=HEADS)
                        q_chain.link(dve, v.tensor_reduce(qsum[:, g.slot, 0, :], flat, AX, ALU.add))
                        q_chain.link(dve, v.reciprocal(qsum[:, g.slot, 1, :], qsum[:, g.slot, 0, :]))
                        q_chain.end()
                        dve.wait_ge(l3_qt.sem, l3_qt.room(g.n))
                        v.tensor_tensor(qs[:, g.slot, :, :].rearrange("p u (h d) -> p (u h) d", h=HEADS), flat,
                                        qsum[:, g.slot, 1, :].unsqueeze(2).broadcast_to([P, GT * HEADS, DH]),
                                        ALU.mult).then_inc(l3_qsoft.sem, 1)

                pipeline(dve, im, 5, l3, left=2)
                k_chain.start(im)
                kc_ = k_chain

                def l3_keys(at):
                    g = at(0)
                    if g is not None:
                        dve.wait_ge(l3_kturned.sem, l3_kturned.after(g.n))
                        dve.wait_ge(l3_ctx.sem, l3_ctx.room(g.n))
                        v.tensor_copy(kt[:, g.slot, :, :],
                                      PS[:, g.slot, :].rearrange("p (u n) -> p u n", u=GT)).then_inc(l3_kback.sem, 1)

                pipeline(dve, im, 1, l3_keys, behind=l3, behind_stages=5)
                dve.wait_ge(ctx_done.sem, ctx_done.after(im))
                dve.wait_ge(l3_kexp.sem, l3_kexp.after(im * NG + NG - 1))
                kc_.link(dve, v.tensor_reduce(kden[:, 0:1], ksum[:, :, :].rearrange("p g s -> p (g s)"), AX, ALU.add))
                kc_.link(dve, v.reciprocal(kden[:, 1:2], kden[:, 0:1]))
                kc_.link(dve, v.tensor_scalar(kden[:, 0:1], kden[:, 1:2], KAPPA * DH ** -0.5, None, ALU.mult))
                for h in range(HEADS):
                    hh = slice(h * DH, (h + 1) * DH)
                    last = v.tensor_scalar(ctxd[hh, hh], PS[hh, 4, hh], kden[hh, 0:1], None, ALU.mult)
                last.then_inc(ctxd_ready.sem, 1)
                dve.wait_ge(ctxt_ps.sem, ctxt_ps.after(im))
                v.tensor_copy(ctxt[:, :], PS[:, 6, 0:P]).then_inc(ctxt_ready.sem, 1)
                dve.wait_ge(mhi_ready.sem, mhi_ready.after(im))
                v.tensor_tensor(m_lo[:, :], PS[:, 5, 0:C], m_hi[:, :], ALU.subtract).then_inc(mlo_ready.sem, 1)
                kc_.end()
                barrier(dve, im, 6)

                def final(at):
                    g = at(2)
                    if g is not None:
                        dve.wait_ge(f_rstd.sem, f_rstd.after(g.n))
                        for u in range(GT):
                            last = v.scalar_tensor_tensor(out=Y[:, g.slot, u, :], in0=z_ps(g)[:, u, :],
                                                          scalar=rstd[:, g.slot, 1, u:u + 1], in1=gamma_b[:, :],
                                                          op0=ALU.mult, op1=ALU.mult)
                        last.then_inc(f_y.sem, 1)
                    g = at(1)
                    if g is not None:
                        dve.wait_ge(f_sq.sem, f_sq.after(g.n))
                        v.tensor_scalar(rstd[:, g.slot, 0, :], sq[:, g.slot, :], 1.0 / C, LN_EPS * KAPPA * KAPPA,
                                        ALU.mult, ALU.add).then_inc(f_ve.sem, 1)
                    g = at(2)
                    if g is not None:
                        dve.wait_ge(f_y.sem, f_y.after(g.n))
                        dve.wait_ge(f_turned.sem, f_turned.after(g.n))
                        dve.wait_ge(stored[g.slot], 16 * (g.occ + 1))
                        v.tensor_tensor(yout[:, g.slot, :, :], Y[:, g.slot, :, :], xt_ps(g),
                                        ALU.add).then_inc(f_out.sem, 1)

                pipeline(dve, im, 3, final)
                barrier(dve, im, 7)

        @block.tensor
        def _(pe):
            mm, tr = nc.tensor.matmul, nc.tensor.transpose

            def split(dst, l_hi, l_lo, r_hi, r_lo, first, last):
                for j, (a, b) in enumerate(((l_hi, r_hi), (l_hi, r_lo), (l_lo, r_hi))):
                    ins = mm(dst, a, b, start=first and j == 0, stop=last and j == 2)
                return ins

            pe.wait_ge(emb_squared, 1)
            for b in range(2):
                for k in range(KC):
                    ins = mm(PS[0:96, b, :], minus_half[:, :], emb_q[:, k, b * 512:(b + 1) * 512],
                             start=k == 0, stop=k == KC - 1)
            ins.then_inc(setup_pe, 1)
            pe.wait_ge(start, 4)

            with pe.Fori(0, B) as im:
                def gn(layer):
                    r = im * 4 + layer
                    pe.wait_ge(mean_ready.sem, mean_ready.after(r))
                    mm(PS[:, 7, 0:KC], gmat[:, :], dm[:, :], start=True, stop=True).then_inc(mean_ps.sem, 1)
                    pe.wait_ge(var_ready.sem, var_ready.after(r))
                    mm(PS[:, 7, 4:4 + KC], gmat[:, :], vv[:, :], start=True, stop=True).then_inc(var_ps.sem, 1)

                for s in range(NG):
                    n = im * NG + s
                    b = 2 * (s % 2)
                    pe.wait_ge(loaded[s], (im + 1) * 16)
                    pe.wait_ge(a_kept.sem, a_kept.room(n))
                    for u in range(GT):
                        for k in range(KC):
                            ins = tr(PS[:, b + k, u * P:(u + 1) * P], xin[:, s, u, k * P:(k + 1) * P], ident[:, :])
                    ins.then_inc(a_turned.sem, 1)
                barrier(pe, im, 0)
                gn(0)

                def l0(at):
                    g, old = at(1), at(2)
                    for u in range(GT):
                        if g is not None:
                            if u == 0:
                                pe.wait_ge(l0_lo.sem, l0_lo.after(g.n))
                            t = g.n * GT + u
                            cols = slice(u * P, (u + 1) * P)
                            pe.wait_ge(l0_indexed.sem, l0_indexed.room(t))
                            for b in range(2):
                                dst = PS[:, 2 * (u % 2) + b, :]
                                half = slice(b * 512, (b + 1) * 512)
                                mm(dst, onesel[:, 0:P], e_bias[:, half], start=True, stop=False)
                                for k in range(KC):
                                    ins = split(dst, xhi[:, g.slot, k, cols], xlo[:, g.slot, k, cols],
                                                e_hi[:, k, half], e_lo[:, k, half], False, k == KC - 1)
                            ins.then_inc(l0_scored.sem, 1)
                        if old is not None:
                            if u == 0:
                                pe.wait_ge(l0_added.sem, l0_added.room(old.n))
                            pe.wait_ge(gathered[old.slot][u], (old.occ + 1) * 16)
                            for k in range(KC):
                                ins = tr(PS[:, 4 + 2 * old.slot + k, u * P:(u + 1) * P],
                                         quant[:, old.slot, u, k * P:(k + 1) * P], ident[:, :])
                            if u == GT - 1:
                                ins.then_inc(l0_turned.sem, 1)

                pipeline(pe, im, 3, l0)
                barrier(pe, im, 1)
                gn(1)

                def l1(at):
                    g = at(1)
                    if g is not None:
                        pe.wait_ge(l1_lo.sem, l1_lo.after(g.n))
                        pe.wait_ge(l1_fgkept.sem, l1_fgkept.room(g.n))
                        products = [(fg_bias, None)]
                        for k in range(KC):
                            products += [(fg_hi[:, k, :], xhi[:, g.slot, k, :]), (fg_hi[:, k, :], xlo[:, g.slot, k, :]),
                                         (fg_lo[:, k, :], xhi[:, g.slot, k, :])]
                        for j, (weight, part) in enumerate(products):
                            for w in range(2):
                                rhs = onesel[:, 0:2 * P] if part is None else part[:, w * 2 * P:(w + 1) * 2 * P]
                                ins = mm(PS[64 * w:64 * w + 64, g.slot, 0:2 * P], weight[:, 0:2 * CK], rhs,
                                         start=j == 0, stop=j == len(products) - 1)
                        ins.then_inc(l1_fg.sem, 1)
                        for w in range(2):
                            pe.wait_ge(l1_hkept.sem, l1_hkept.room(g.n * 2 + w))
                            for u in range(2):
                                cols = slice((2 * w + u) * P, (2 * w + u + 1) * P)
                                for k in range(KC):
                                    ins = split(PS[:, 4 + w, u * C:(u + 1) * C], xhi[:, g.slot, k, cols],
                                                xlo[:, g.slot, k, cols], h_hi[:, k, :], h_lo[:, k, :],
                                                k == 0, k == KC - 1)
                            ins.then_inc(l1_h.sem, 1)
                        pe.wait_ge(l1_fgkept.sem, l1_fgkept.after(g.n))
                        pe.wait_ge(l1_tanh.sem, l1_tanh.room(g.n))
                        for u in range(GT):
                            cols = slice(u % 2 * P, (u % 2 + 1) * P)
                            ins = mm(PS[:, 2 + g.slot, u * P:(u + 1) * P], GTm[:, g.slot, u // 2, cols],
                                     FT[:, g.slot, u // 2, cols], start=True, stop=True)
                        ins.then_inc(l1_scores.sem, 1)
                    g = at(2)
                    if g is not None:
                        pe.wait_ge(l1_attn.sem, l1_attn.after(g.n))
                        pe.wait_ge(l1_hkept.sem, l1_hkept.after(g.n * 2 + 1))
                        pe.wait_ge(l1_added.sem, l1_added.room(g.n))
                        for k in range(KC):
                            for u in range(GT):
                                ins = mm(PS[:, 6 + k, u * P:(u + 1) * P], H[:, g.slot, u, k * P:(k + 1) * P],
                                         attn[:, g.slot, u, :], start=True, stop=True)
                        ins.then_inc(l1_out.sem, 1)

                pipeline(pe, im, 3, l1)
                barrier(pe, im, 2)
                gn(2)

                pe.wait_ge(gn_ready.sem, gn_ready.after(im * 4 + 2))
                for k in range(KC):
                    ins = mm(PS[:, 2, 0:1], w3_sb[:, k, :], gt[:, k:k + 1], start=k == 0, stop=k == KC - 1)
                ins.then_inc(pb3_ps.sem, 1)
                pe.wait_ge(w3_scaled.sem, w3_scaled.after(im))
                pe.wait_ge(pb3_ready.sem, pb3_ready.after(im))
                for b in range(2):
                    for k in range(KC):
                        for q in range(QUADS):
                            ins = mm(PS[32 * q:32 * q + 32, b, :], w3s[:, k, :], XT[:, k, 2 * b + q // 2, q % 2, :],
                                     start=k == 0, stop=k == KC - 1)
                    ins.then_inc(l2_proj.sem, 1)
                for b in range(2):
                    pe.wait_ge(l2_rows.sem, l2_rows.after(im * 2 + b))
                    for j in range(GT):
                        ins = tr(PS[:, 4 + b, j * P:(j + 1) * P], rows3[:, b, j * P:(j + 1) * P], ident[:, :])
                ins.then_inc(rows_turned.sem, 1)
                pe.wait_ge(x0max_in.sem, x0max_in.after(im))
                tr(PS[0:2, 0, 0:P], mm2[:, :], ident[:, :]).then_inc(x0max_t.sem, 1)
                pe.wait_ge(x0max_d.sem, x0max_d.after(im))
                mm(PS[:, 1, 0:2], ones[0:2, :], dg2[:, :], start=True, stop=True).then_inc(x0max_b.sem, 1)
                pe.wait_ge(pieces_made.sem, pieces_made.after(im))
                for s in range(NG):
                    n = im * NG + s
                    pe.wait_ge(lhs_kept.sem, lhs_kept.room(n))
                    pe.wait_ge(rhs_kept.sem, rhs_kept.room(n))
                    apart(pe)
                    for u in range(GT):
                        ins = tr(PS[0:44, s % 4, u * P:(u + 1) * P], pc[:, s * GT + u, :], ident[:, :])
                    ins.then_inc(pieces_turned.sem, 1)
                barrier(pe, im, 3)

                for f in range(NHALF):
                    for q in range(QUADS):
                        mm(PS[32 * q:32 * q + 32, 6 + f, :], zero_w[:, 0:32], xn[:, 0, 0, :], start=True, stop=False,
                           skip_group_check=True)

                def fill(i, tt, z):
                    c = (im * NT + i * TRIO + tt) * 4 + z
                    zone = (tt * 4 + z) % ZONES
                    if z == 0:
                        pe.wait_ge(tile_staged.sem, tile_staged.after(im * NT + i * TRIO + tt))
                    pe.wait_ge(exps_done.sem, exps_done.room(c))
                    for b in range(2):
                        m0 = z * ZW + b * 512
                        ins = mm(PS[:, 2 * zone + b, :], lhs_s[:, tt % TRIO, :], rhs_p[:, m0:m0 + 512],
                                 start=True, stop=True)
                    ins.then_inc(exps_in.sem, 1)

                def sums(i, tt, f, close=False):
                    t = im * NT + i * TRIO + tt
                    e = (tt * 2 + f) % TRIO
                    pe.wait_ge(exps_done.sem, exps_done.after(t * 4 + 2 * f + 1))
                    for q in range(QUADS):
                        ins = mm(PS[32 * q:32 * q + 32, 6 + f, :], w2[:, tt % TRIO, :], E[:, e, q * 512:(q + 1) * 512],
                                 start=False, stop=close, skip_group_check=True)
                    ins.then_inc(sums_done.sem, 1)

                body = NT // TRIO
                rest = NT - body * TRIO
                fill(0, 0, 0)
                fill(0, 0, 1)

                def half_step(i, tt, f, nxt, close=False):
                    if nxt is not None:
                        fill(*nxt)
                        fill(nxt[0], nxt[1], nxt[2] + 1)
                    sums(i, tt, f, close)

                with pe.Fori(0, body) as i:
                    for tt in range(TRIO):
                        half_step(i, tt, 0, (i, tt, 2))
                        half_step(i, tt, 1, (i, tt + 1, 0))
                for tt in range(rest):
                    half_step(body, tt, 0, (body, tt, 2), tt == rest - 1)
                    half_step(body, tt, 1, (body, tt + 1, 0) if tt < rest - 1 else None, tt == rest - 1)
                pe.wait_ge(acc_kept.sem, acc_kept.after(im))
                for f in range(NHALF):
                    for j in range(GT):
                        ins = tr(PS[:, f, j * P:(j + 1) * P], accs[:, f * 512 + j * P:f * 512 + (j + 1) * P], ident[:, :])
                ins.then_inc(acc_turned.sem, 1)
                barrier(pe, im, 4)

                def l2_spread(at):
                    g = at(0)
                    if g is not None:
                        pe.wait_ge(g_diag.sem, g_diag.after(g.n))
                        pe.wait_ge(g_diag_last.sem, g_diag_last.after(g.n))
                        pe.wait_ge(g_gated.sem, g_gated.room(g.n))
                        mm(PS[:, g.slot, :], ones[:, :], diag[:, g.slot, :, :].rearrange("p u n -> p (u n)"),
                           start=True, stop=True).then_inc(g_spread.sem, 1)

                pipeline(pe, im, 1, l2_spread)
                barrier(pe, im, 5)
                gn(3)

                def l3(at):
                    g = at(4)
                    if g is not None:
                        pe.wait_ge(l3_qsoft.sem, l3_qsoft.after(g.n))
                        pe.wait_ge(l3_qlo.sem, l3_qlo.room(g.n))
                        for u in range(GT):
                            ins = tr(PS[:, 6 + g.slot, u * P:(u + 1) * P], qs[:, g.slot, u, :], ident[:, :])
                        ins.then_inc(l3_qt.sem, 1)
                    g = at(1)
                    if g is not None:
                        pe.wait_ge(l3_lo.sem, l3_lo.after(g.n))
                        pe.wait_ge(l3_kkept.sem, l3_kkept.room(g.n))
                        for k in range(KC):
                            ins = split(PS[:, g.slot, :], k_hi[:, k, :], k_lo[:, k, :], xhi[:, g.slot, k, :],
                                        xlo[:, g.slot, k, :], k == 0, k == KC - 1)
                        ins.then_inc(l3_k.sem, 1)
                        pe.wait_ge(l3_vkept.sem, l3_vkept.room(g.n))
                        pe.wait_ge(l3_qsub.sem, l3_qsub.room(g.n))
                        for u in range(GT):
                            cols = slice(u * P, (u + 1) * P)
                            for k in range(KC):
                                ins = split(qv_ps(g)[:, u, :], xhi[:, g.slot, k, cols], xlo[:, g.slot, k, cols],
                                            qv_hi[:, k, :], qv_lo[:, k, :], k == 0, k == KC - 1)
                        ins.then_inc(l3_qv.sem, 1)

                pipeline(pe, im, 5, l3, left=2)

                pe.wait_ge(l3_qsub.sem, l3_qsub.after(im * NG + NG - 1))
                pe.wait_ge(l3_vkept.sem, l3_vkept.after(im * NG + NG - 1))
                mm(PS[:, 4, 0:P], zero_w[:, :], ident[:, :], start=True, stop=False, skip_group_check=True)

                def l3_keys(at):
                    g = at(0)
                    if g is not None:
                        pe.wait_ge(l3_kexp.sem, l3_kexp.after(g.n))
                        pe.wait_ge(l3_kback.sem, l3_kback.room(g.n))
                        for u in range(GT):
                            ins = tr(PS[:, g.slot, u * P:(u + 1) * P], ke[:, g.slot, u, :], ident[:, :])
                        ins.then_inc(l3_kturned.sem, 1)
                    g = at(1)
                    if g is not None:
                        pe.wait_ge(l3_kback.sem, l3_kback.after(g.n))
                        for u in range(GT):
                            ins = mm(PS[:, 4, 0:P], kt[:, g.slot, u, :], V[:, g.pair, g.slot, u, :],
                                     start=False, stop=False, skip_group_check=True)
                        ins.then_inc(l3_ctx.sem, 1)

                pipeline(pe, im, 2, l3_keys, behind=l3, behind_stages=5)
                mm(PS[:, 4, 0:P], zero_w[:, :], ident[:, :], start=False, stop=True,
                   skip_group_check=True).then_inc(ctx_done.sem, 1)
                pe.wait_ge(ctxd_ready.sem, ctxd_ready.after(im))
                tr(PS[:, 6, 0:P], ctxd[:, :], ident[:, :]).then_inc(ctxt_ps.sem, 1)
                pe.wait_ge(ctxt_ready.sem, ctxt_ready.after(im))
                mm(PS[:, 5, 0:C], ctxt[:, :], wo_c[:, :], start=True, stop=True).then_inc(m_ps.sem, 1)
                barrier(pe, im, 6)

                def final(at):
                    g = at(1)
                    if g is not None:
                        pe.wait_ge(f_y.sem, f_y.room(g.n))
                        for u in range(GT):
                            dst = z_ps(g)[:, u, :]
                            mm(dst, onesel[:, 0:P], z_bias[:, :], start=True, stop=False)
                            ins = split(dst, q_hi[:, g.pair, g.slot, u, :], q_lo[:, g.pair, g.slot, u, :],
                                        m_hi[:, :], m_lo[:, :], False, True)
                        ins.then_inc(f_z.sem, 1)
                    g = at(2)
                    if g is not None:
                        pe.wait_ge(f_xb.sem, f_xb.after(g.n))
                        pe.wait_ge(f_out.sem, f_out.room(g.n))
                        for u in range(GT):
                            for k in range(KC):
                                ins = tr(xt_ps(g)[:, u, k * P:(k + 1) * P], xb[:, g.slot, k, u * P:(u + 1) * P],
                                         ident[:, :])
                        ins.then_inc(f_turned.sem, 1)

                pipeline(pe, im, 3, final)
                barrier(pe, im, 7)


def kernel(x, L0_conv_embeddings, L1_conv_Wf, L1_conv_bf, L1_conv_Wg, L1_conv_bg, L1_conv_Wh, L1_conv_bh,
           L2_conv_w1, L2_conv_b1, L2_conv_w2, L2_conv_b2, L2_conv_w3, L2_conv_b3,
           L3_conv_w_qkv, L3_conv_w_out, L3_conv_b_out, L3_conv_gamma, L3_conv_beta):
    import numpy as np
    import concourse.bacc as bacc
    from concourse.bass_utils import run_bass_kernel_spmd

    emb = np.asarray(L0_conv_embeddings)
    qkv = np.asarray(L3_conv_w_qkv)

    def in_strips(v):
        laid = np.zeros((v.shape[1], QUADS, 32), v.dtype)
        laid[:, :, 0:3] = v.T[:, None, :]
        return laid.reshape(v.shape[1], P)

    arrays = dict(
        x=np.asarray(x),
        emb=emb,
        emb_t=emb.T,
        wfg=np.concatenate([np.asarray(L1_conv_Wf), np.asarray(L1_conv_Wg)], axis=1),
        bfg=np.concatenate([np.asarray(L1_conv_bf), np.asarray(L1_conv_bg)]),
        wh=np.asarray(L1_conv_Wh),
        bh=np.asarray(L1_conv_bh),
        w3=in_strips(np.stack([np.asarray(L2_conv_w1), np.asarray(L2_conv_w2), np.asarray(L2_conv_w3)])),
        b3=in_strips(np.stack([np.asarray(L2_conv_b1), np.asarray(L2_conv_b2), np.asarray(L2_conv_b3)])).T,
        wqv=np.concatenate([qkv[:, 0:HID], qkv[:, 2 * HID:3 * HID]], axis=1),
        wk=qkv[:, HID:2 * HID],
        w_out=np.asarray(L3_conv_w_out),
        b_out=np.asarray(L3_conv_b_out),
        gamma=np.asarray(L3_conv_gamma),
        beta=np.asarray(L3_conv_beta).reshape(KC, P).T,
        ident_in=np.eye(P, dtype=np.float32),
        gmat_in=np.kron(np.eye(P // GN_GROUP, dtype=np.float32),
                        np.full((GN_GROUP, GN_GROUP), 1.0 / GN_GROUP, np.float32)),
    )
    nc = bacc.Bacc("TRN2", target_bir_lowering=False, num_devices=1)
    feeds, args = {}, []
    for name, a in arrays.items():
        a = np.ascontiguousarray(a)
        feeds[name] = a
        args.append(nc.dram_tensor(name, a.shape, mybir.dt.from_np(a.dtype), kind="ExternalInput").ap())
    out = nc.dram_tensor("out", arrays["x"].shape, F32, kind="ExternalOutput").ap()
    build(nc, *args, out)
    return run_bass_kernel_spmd(nc, [feeds], core_ids=[0]).results[0]["out"]
```
